# Optimizing a Trainium2 kernel written in Bass

```python
import numpy as np
import jax
import jax.numpy as jnp

def _softmax(x, axis=-1):
    return jax.nn.softmax(x, axis=axis)

def _gelu(x):
    return jax.nn.gelu(x, approximate=True)

def _silu(x):
    return jax.nn.silu(x)

def _sigmoid(x):
    return jax.nn.sigmoid(x)

def _layernorm(x, axis=-1, eps=1e-05):
    m = jnp.mean(x, axis=axis, keepdims=True)
    v = jnp.var(x, axis=axis, keepdims=True)
    return (x - m) / jnp.sqrt(v + eps)

def _scatter_add(tgt, idx, src, axis=0):
    return tgt.at[idx].add(src)

def _segment_sum(src, seg, n):
    return jax.ops.segment_sum(src, seg, n)
kernel_name = 'mk_vit_tower_postln_d2_tok_img256_r4_874b51'

def setup_inputs(seed: int=0):
    np.random.seed(seed)
    _w = jnp.asarray

    def _rec_inputs():
        import jax
        import jax.numpy as jnp
        _rk = jax.random.key(seed)
        x = -0.000520686 + 1.00062 * jax.random.normal(jax.random.fold_in(_rk, 1), (128, 64, 64, 4), jnp.float32)
        return x
    x = _rec_inputs()

    def _L0_tok_setup():
        import jax, jax.numpy as jnp
        import numpy as np
        HIDDEN_DIM = 128
        key = jax.random.key(seed)
        k_geom, k_w, k_b = jax.random.split(key, 3)
        B, N, F = (8, 64, 4)
        geom = jax.random.normal(k_geom, (B, N, N, F), dtype=jnp.float32)
        bound = 1.0 / np.sqrt(F)
        W = jax.random.uniform(k_w, (HIDDEN_DIM, F), dtype=jnp.float32, minval=-bound, maxval=bound)
        b = jax.random.uniform(k_b, (HIDDEN_DIM,), dtype=jnp.float32, minval=-bound, maxval=bound)
        return {'geom': geom, 'W': W, 'b': b}
    _L0_tok_all = _L0_tok_setup()
    _L0_tok_in = {k: v for k, v in _L0_tok_all.items() if k in ('W', 'b')}
    del _L0_tok_all

    def _L0_attn_setup():
        import jax, jax.numpy as jnp
        import numpy as np
        D_MODEL = 64
        EXPAND = 2
        D_STATE = 8
        E = D_MODEL * EXPAND
        BATCH = 8
        SEQ = 512
        BN_EPS = 1e-05
        key = jax.random.key(seed)
        ks = jax.random.split(key, 8)
        x = jax.random.normal(ks[0], (BATCH, SEQ, D_MODEL), jnp.float32)
        w1 = jax.random.normal(ks[1], (E, D_MODEL), jnp.float32) * 0.05
        b1 = jnp.zeros((E,), jnp.float32)
        wd = jax.random.normal(ks[2], (E, 1, 5), jnp.float32) * 0.1
        bd = jnp.zeros((E,), jnp.float32)
        gamma = jnp.ones((E,), jnp.float32)
        beta = jnp.zeros((E,), jnp.float32)
        rmean = jnp.zeros((E,), jnp.float32)
        rvar = jnp.ones((E,), jnp.float32)
        A = -jnp.ones((E,), jnp.float32) * 0.5
        Bm = jax.random.normal(ks[3], (E, D_STATE), jnp.float32) * 0.1
        Cm = jax.random.normal(ks[4], (E, D_STATE), jnp.float32) * 0.1
        Dv = jax.random.normal(ks[5], (E,), jnp.float32) * 0.1
        w2 = jax.random.normal(ks[6], (D_MODEL, E), jnp.float32) * 0.05
        b2 = jnp.zeros((D_MODEL,), jnp.float32)
        return dict(x=x, w1=w1, b1=b1, wd=wd, bd=bd, gamma=gamma, beta=beta, rmean=rmean, rvar=rvar, A=A, Bm=Bm, Cm=Cm, Dv=Dv, w2=w2, b2=b2)
    _L0_attn_all = _L0_attn_setup()
    _L0_attn_in = {k: v for k, v in _L0_attn_all.items() if k in ('w1', 'b1', 'wd', 'bd', 'gamma', 'beta', 'rmean', 'rvar', 'A', 'Bm', 'Cm', 'Dv', 'w2', 'b2')}
    del _L0_attn_all

    def _L0_ffn_setup():
        import jax, jax.numpy as jnp
        import numpy as np
        DIM = 64
        HEADS = 8
        NUM_KEYS = 64
        NUM_KV = NUM_KEYS ** 2
        PK_TOPK = 16
        FINAL_TOPK = 16
        DIM_KEY = DIM // 2
        P = 2

        def _pk(x, Wq_pk, pk_keys):
            b, n, _ = x.shape
            q = (x @ Wq_pk).reshape(b, n, P, HEADS, DIM_KEY).transpose(2, 0, 1, 3, 4)
            sim = jnp.einsum('pbnhd,pkhd->pbnhk', q, pk_keys)
            scores, idx = jax.lax.top_k(sim, PK_TOPK)
            idx0 = idx[0]
            idx1 = idx[1] * NUM_KEYS
            index = (idx0[..., :, None] + idx1[..., None, :]).reshape(b, n, HEADS, PK_TOPK * PK_TOPK)
            score = (scores[0][..., :, None] + scores[1][..., None, :]).reshape(b, n, HEADS, PK_TOPK * PK_TOPK)
            final_scores, pk_idx = jax.lax.top_k(score, FINAL_TOPK)
            final_indices = jnp.take_along_axis(index, pk_idx, axis=-1)
            final_scores = jax.nn.softmax(final_scores, axis=-1)
            return (final_scores, final_indices)
        key = jax.random.key(seed)
        ks = jax.random.split(key, 7)
        b, n = (2, 256)
        std = 0.02
        x = jax.random.normal(ks[0], (b, n, DIM), dtype=jnp.float32)
        Wq_pk = jax.random.normal(ks[1], (DIM, P * HEADS * DIM_KEY), dtype=jnp.float32) * std
        pk_keys = jax.random.normal(ks[2], (P, NUM_KEYS, HEADS, DIM_KEY), dtype=jnp.float32) * std
        Wq = jax.random.normal(ks[3], (DIM, HEADS * DIM), dtype=jnp.float32) * std
        keys_table = jax.random.normal(ks[4], (NUM_KV * HEADS, DIM), dtype=jnp.float32) * std
        values_table = jax.random.normal(ks[5], (NUM_KV * HEADS, DIM), dtype=jnp.float32) * std
        Wo = jax.random.normal(ks[6], (DIM * HEADS, DIM), dtype=jnp.float32) * std
        return {'x': x, 'Wq_pk': Wq_pk, 'pk_keys': pk_keys, 'Wq': Wq, 'keys_table': keys_table, 'values_table': values_table, 'Wo': Wo}
    _L0_ffn_all = _L0_ffn_setup()
    _L0_ffn_in = {k: v for k, v in _L0_ffn_all.items() if k in ('Wq_pk', 'pk_keys', 'Wq', 'keys_table', 'values_table', 'Wo')}
    del _L0_ffn_all

    def _L1_attn_setup():
        import jax, jax.numpy as jnp
        import numpy as np
        B, L, H, N = (16, 2048, 64, 128)

        def _lru_forward(inputs, Wi, bi, Wo, bo, params_log):
            b, l_seq, _ = inputs.shape
            n = params_log.shape[1]
            u = inputs @ Wi.T + bi
            params = jnp.exp(params_log)
            nu, theta, gamma = (params[0], params[1], params[2])
            u_c = jax.lax.complex(u[..., :n], u[..., n:])
            log2_L = int(np.ceil(np.log2(l_seq)))
            P = 2 ** log2_L
            x = jnp.pad(u_c, ((0, 0), (0, P - l_seq), (0, 0)))
            for i in range(1, log2_L + 1):
                l = 2 ** i
                x = x.reshape(b * P // l, l, n)
                x1, x2 = (x[:, :l // 2], x[:, l // 2:])
                pos = jnp.arange(1, l // 2 + 1, dtype=jnp.float32)
                lambs = jnp.exp(jax.lax.complex(-pos[:, None] * nu, pos[:, None] * theta))
                x2 = x2 + lambs * x1[:, -1:]
                x = jnp.concatenate([x1, x2], axis=1).reshape(b, P, n)
            x = x[:, :l_seq] * gamma
            y = jnp.concatenate([jnp.real(x), jnp.imag(x)], axis=-1)
            return y @ Wo.T + bo
        key = jax.random.key(seed)
        k = jax.random.split(key, 5)
        inputs = jax.random.normal(k[0], (B, L, H), dtype=jnp.float32)
        Wi = jax.random.normal(k[1], (2 * N, H), dtype=jnp.float32) / np.sqrt(H).astype(np.float32)
        bi = jnp.zeros((2 * N,), jnp.float32)
        Wo = jax.random.normal(k[2], (H, 2 * N), dtype=jnp.float32) / np.sqrt(2 * N).astype(np.float32)
        bo = jnp.zeros((H,), jnp.float32)
        r_min, r_max = (0.9, 0.999)
        u1 = jax.random.uniform(k[3], (N,), dtype=jnp.float32)
        u2 = jax.random.uniform(k[4], (N,), dtype=jnp.float32)
        nu_log = jnp.log(-0.5 * jnp.log(u1 * (r_max ** 2 - r_min ** 2) + r_min ** 2))
        theta_log = jnp.log(u2 * 2.0 * np.pi)
        gamma_log = jnp.log(jnp.sqrt(1.0 - jnp.exp(-jnp.exp(nu_log)) ** 2))
        params_log = jnp.stack([nu_log, theta_log, gamma_log])
        return {'inputs': inputs, 'Wi': Wi, 'bi': bi, 'Wo': Wo, 'bo': bo, 'params_log': params_log}
    _L1_attn_all = _L1_attn_setup()
    _L1_attn_in = {k: v for k, v in _L1_attn_all.items() if k in ('Wi', 'bi', 'Wo', 'bo', 'params_log')}
    del _L1_attn_all

    def _L1_ffn_setup():
        import jax, jax.numpy as jnp
        import numpy as np
        B, S, H, F, E, K = (8, 1024, 64, 128, 16, 2)
        EPS = 1e-05
        key = jax.random.key(seed)
        ks = jax.random.split(key, 9)
        sc = 0.02
        return {'x': jax.random.normal(ks[0], (B, S, H), dtype=jnp.float32), 'gate_w': jax.random.normal(ks[1], (H, E), dtype=jnp.float32) * sc, 'gate_b': jnp.zeros((E,), dtype=jnp.float32), 'w1': jax.random.normal(ks[2], (E, H, F), dtype=jnp.float32) * sc, 'b1': jnp.zeros((E, F), dtype=jnp.float32), 'w2': jax.random.normal(ks[3], (E, F, H), dtype=jnp.float32) * sc, 'b2': jnp.zeros((E, H), dtype=jnp.float32), 'gamma': jnp.ones((H,), dtype=jnp.float32), 'beta': jnp.zeros((H,), dtype=jnp.float32)}
    _L1_ffn_all = _L1_ffn_setup()
    _L1_ffn_in = {k: v for k, v in _L1_ffn_all.items() if k in ('gate_w', 'gate_b', 'w1', 'b1', 'w2', 'b2', 'gamma', 'beta')}
    del _L1_ffn_all
    return {'x': x, 'L0_tok_W': _L0_tok_in['W'], 'L0_tok_b': _L0_tok_in['b'], 'L0_attn_w1': _L0_attn_in['w1'], 'L0_attn_b1': _L0_attn_in['b1'], 'L0_attn_wd': _L0_attn_in['wd'], 'L0_attn_bd': _L0_attn_in['bd'], 'L0_attn_gamma': _L0_attn_in['gamma'], 'L0_attn_beta': _L0_attn_in['beta'], 'L0_attn_rmean': _L0_attn_in['rmean'], 'L0_attn_rvar': _L0_attn_in['rvar'], 'L0_attn_A': _L0_attn_in['A'], 'L0_attn_Bm': _L0_attn_in['Bm'], 'L0_attn_Cm': _L0_attn_in['Cm'], 'L0_attn_Dv': _L0_attn_in['Dv'], 'L0_attn_w2': _L0_attn_in['w2'], 'L0_attn_b2': _L0_attn_in['b2'], 'L0_ffn_Wq_pk': _L0_ffn_in['Wq_pk'], 'L0_ffn_pk_keys': _L0_ffn_in['pk_keys'], 'L0_ffn_Wq': _L0_ffn_in['Wq'], 'L0_ffn_keys_table': _L0_ffn_in['keys_table'], 'L0_ffn_values_table': _L0_ffn_in['values_table'], 'L0_ffn_Wo': _L0_ffn_in['Wo'], 'L1_attn_Wi': _L1_attn_in['Wi'], 'L1_attn_bi': _L1_attn_in['bi'], 'L1_attn_Wo': _L1_attn_in['Wo'], 'L1_attn_bo': _L1_attn_in['bo'], 'L1_attn_params_log': _L1_attn_in['params_log'], 'L1_ffn_gate_w': _L1_ffn_in['gate_w'], 'L1_ffn_gate_b': _L1_ffn_in['gate_b'], 'L1_ffn_w1': _L1_ffn_in['w1'], 'L1_ffn_b1': _L1_ffn_in['b1'], 'L1_ffn_w2': _L1_ffn_in['w2'], 'L1_ffn_b2': _L1_ffn_in['b2'], 'L1_ffn_gamma': _L1_ffn_in['gamma'], 'L1_ffn_beta': _L1_ffn_in['beta']}

def reference(x, L0_tok_W, L0_tok_b, L0_attn_w1, L0_attn_b1, L0_attn_wd, L0_attn_bd, L0_attn_gamma, L0_attn_beta, L0_attn_rmean, L0_attn_rvar, L0_attn_A, L0_attn_Bm, L0_attn_Cm, L0_attn_Dv, L0_attn_w2, L0_attn_b2, L0_ffn_Wq_pk, L0_ffn_pk_keys, L0_ffn_Wq, L0_ffn_keys_table, L0_ffn_values_table, L0_ffn_Wo, L1_attn_Wi, L1_attn_bi, L1_attn_Wo, L1_attn_bo, L1_attn_params_log, L1_ffn_gate_w, L1_ffn_gate_b, L1_ffn_w1, L1_ffn_b1, L1_ffn_w2, L1_ffn_b2, L1_ffn_gamma, L1_ffn_beta):
    import jax
    import jax.numpy as jnp

    def _L0_tok_ref(geom, W, b):
        import jax, jax.numpy as jnp
        import numpy as np
        HIDDEN_DIM = 128
        bias = jnp.einsum('bijf,hf->bijh', geom, W) + b
        return bias.mean(-1)

    def _L0_attn_ref(x, w1, b1, wd, bd, gamma, beta, rmean, rvar, A, Bm, Cm, Dv, w2, b2):
        import jax, jax.numpy as jnp
        import numpy as np
        D_MODEL = 64
        EXPAND = 2
        D_STATE = 8
        E = D_MODEL * EXPAND
        BATCH = 8
        SEQ = 512
        BN_EPS = 1e-05
        xc = jax.nn.silu(jnp.einsum('bld,ed->ble', x, w1) + b1)
        xcc = jnp.transpose(xc, (0, 2, 1))
        y = jax.lax.conv_general_dilated(xcc, wd, window_strides=(1,), padding=[(2, 2)], dimension_numbers=('NCH', 'OIH', 'NCH'), feature_group_count=E)
        y = y + bd[None, :, None]
        scale = gamma * jax.lax.rsqrt(rvar + BN_EPS)
        y = y * scale[None, :, None] + (beta - rmean * scale)[None, :, None]
        y = jax.nn.silu(y)
        x_local = jnp.transpose(y, (0, 2, 1))
        expA = jnp.exp(A)

        def step(h, xt):
            h = expA[None, :, None] * h + xt[:, :, None] * Bm[None]
            yt = jnp.einsum('bes,es->be', h, Cm) + Dv * xt
            return (h, yt)
        h0 = jnp.zeros((x.shape[0], E, D_STATE), x.dtype)
        _, ys = jax.lax.scan(step, h0, jnp.transpose(x_local, (1, 0, 2)))
        out = jnp.transpose(ys, (1, 0, 2))
        out = jnp.einsum('ble,de->bld', out, w2) + b2
        return out

    def _L0_ffn_ref(x, Wq_pk, pk_keys, Wq, keys_table, values_table, Wo):
        import jax, jax.numpy as jnp
        import numpy as np
        DIM = 64
        HEADS = 8
        NUM_KEYS = 64
        NUM_KV = NUM_KEYS ** 2
        PK_TOPK = 16
        FINAL_TOPK = 16
        DIM_KEY = DIM // 2
        P = 2

        def _pk(x, Wq_pk, pk_keys):
            b, n, _ = x.shape
            q = (x @ Wq_pk).reshape(b, n, P, HEADS, DIM_KEY).transpose(2, 0, 1, 3, 4)
            sim = jnp.einsum('pbnhd,pkhd->pbnhk', q, pk_keys)
            scores, idx = jax.lax.top_k(sim, PK_TOPK)
            idx0 = idx[0]
            idx1 = idx[1] * NUM_KEYS
            index = (idx0[..., :, None] + idx1[..., None, :]).reshape(b, n, HEADS, PK_TOPK * PK_TOPK)
            score = (scores[0][..., :, None] + scores[1][..., None, :]).reshape(b, n, HEADS, PK_TOPK * PK_TOPK)
            final_scores, pk_idx = jax.lax.top_k(score, FINAL_TOPK)
            final_indices = jnp.take_along_axis(index, pk_idx, axis=-1)
            final_scores = jax.nn.softmax(final_scores, axis=-1)
            return (final_scores, final_indices)
        b, n, d = x.shape
        q = (x @ Wq).reshape(b, n, HEADS, DIM) * DIM ** (-0.5)
        kv_scores, indices = _pk(x, Wq_pk, pk_keys)
        offsets = jnp.arange(HEADS, dtype=indices.dtype) * NUM_KV
        ind = indices + offsets[None, None, :, None]
        k = jnp.einsum('bnhk,bnhkd->bnhd', kv_scores, keys_table[ind])
        v = jnp.einsum('bnhk,bnhkd->bnhd', kv_scores, values_table[ind])
        sim = jnp.einsum('bihd,bjhd->bhij', q, k)
        neg = -jnp.finfo(sim.dtype).max
        causal = jnp.tril(jnp.ones((n, n), dtype=bool))
        sim = jnp.where(causal, sim, neg)
        attn = jax.nn.softmax(sim, axis=-1)
        out = jnp.einsum('bhij,bjhd->bhid', attn, v)
        out = out.transpose(0, 2, 1, 3).reshape(b, n, HEADS * DIM)
        return out @ Wo

    def _L1_attn_ref(inputs, Wi, bi, Wo, bo, params_log):
        import jax, jax.numpy as jnp
        import numpy as np
        B, L, H, N = (16, 2048, 64, 128)

        def _lru_forward(inputs, Wi, bi, Wo, bo, params_log):
            b, l_seq, _ = inputs.shape
            n = params_log.shape[1]
            u = inputs @ Wi.T + bi
            params = jnp.exp(params_log)
            nu, theta, gamma = (params[0], params[1], params[2])
            u_c = jax.lax.complex(u[..., :n], u[..., n:])
            log2_L = int(np.ceil(np.log2(l_seq)))
            P = 2 ** log2_L
            x = jnp.pad(u_c, ((0, 0), (0, P - l_seq), (0, 0)))
            for i in range(1, log2_L + 1):
                l = 2 ** i
                x = x.reshape(b * P // l, l, n)
                x1, x2 = (x[:, :l // 2], x[:, l // 2:])
                pos = jnp.arange(1, l // 2 + 1, dtype=jnp.float32)
                lambs = jnp.exp(jax.lax.complex(-pos[:, None] * nu, pos[:, None] * theta))
                x2 = x2 + lambs * x1[:, -1:]
                x = jnp.concatenate([x1, x2], axis=1).reshape(b, P, n)
            x = x[:, :l_seq] * gamma
            y = jnp.concatenate([jnp.real(x), jnp.imag(x)], axis=-1)
            return y @ Wo.T + bo
        return _lru_forward(inputs, Wi, bi, Wo, bo, params_log)

    def _L1_ffn_ref(x, gate_w, gate_b, w1, b1, w2, b2, gamma, beta):
        import jax, jax.numpy as jnp
        import numpy as np
        B, S, H, F, E, K = (8, 1024, 64, 128, 16, 2)
        EPS = 1e-05
        gate_logits = x @ gate_w + gate_b
        topk_vals, topk_idx = jax.lax.top_k(gate_logits, K)
        topk_w = jax.nn.softmax(topk_vals, axis=-1)
        h = jax.nn.relu(jnp.einsum('bsh,ehf->bsef', x, w1) + b1)
        expert_out = jnp.einsum('bsef,efh->bseh', h, w2) + b2
        sel = jnp.take_along_axis(expert_out, topk_idx[:, :, :, None], axis=2)
        moe = jnp.sum(topk_w[..., None] * sel, axis=2)
        y = x + moe
        mu = jnp.mean(y, axis=-1, keepdims=True)
        var = jnp.var(y, axis=-1, keepdims=True)
        return (y - mu) / jnp.sqrt(var + EPS) * gamma + beta
    h = _L0_tok_ref(x, L0_tok_W, L0_tok_b)
    h = _layernorm(h + _L0_attn_ref(h, L0_attn_w1, L0_attn_b1, L0_attn_wd, L0_attn_bd, L0_attn_gamma, L0_attn_beta, L0_attn_rmean, L0_attn_rvar, L0_attn_A, L0_attn_Bm, L0_attn_Cm, L0_attn_Dv, L0_attn_w2, L0_attn_b2), axis=-1)
    h = _layernorm(h + _L0_ffn_ref(h, L0_ffn_Wq_pk, L0_ffn_pk_keys, L0_ffn_Wq, L0_ffn_keys_table, L0_ffn_values_table, L0_ffn_Wo), axis=-1)
    h = _layernorm(h + _L1_attn_ref(h, L1_attn_Wi, L1_attn_bi, L1_attn_Wo, L1_attn_bo, L1_attn_params_log), axis=-1)
    h = _layernorm(h + _L1_ffn_ref(h, L1_ffn_gate_w, L1_ffn_gate_b, L1_ffn_w1, L1_ffn_b1, L1_ffn_w2, L1_ffn_b2, L1_ffn_gamma, L1_ffn_beta), axis=-1)
    return h

_drawn_inputs = setup_inputs


def setup_inputs(seed=0):
    import zlib

    import numpy as np

    out = dict(_drawn_inputs(seed))
    spreads = {'L0_attn_b1': (0.0, 0.8),
     'L0_attn_bd': (0.0, 0.338),
     'L0_attn_gamma': (1.0, 0.6),
     'L0_attn_beta': (0.0, 0.369),
     'L0_attn_rmean': (0.0, 0.402),
     'L0_attn_rvar': (1.0, 0.6),
     'L0_attn_A': (-0.5, 0.6),
     'L0_attn_b2': (0.0, 0.1),
     'L1_attn_bi': (0.0, 0.1),
     'L1_attn_bo': (0.0, 0.1),
     'L1_ffn_gate_b': (0.0, 0.325),
     'L1_ffn_b1': (0.0, 0.8),
     'L1_ffn_b2': (0.0, 0.273),
     'L1_ffn_gamma': (1.0, 0.2),
     'L1_ffn_beta': (0.0, 0.1)}
    factors = {'L0_tok_b': 64.0,
     'L0_attn_w1': 8.0,
     'L0_attn_wd': 8.0,
     'L0_attn_Bm': 3.102,
     'L0_attn_Cm': 3.376,
     'L0_ffn_Wq_pk': 8.0,
     'L0_ffn_pk_keys': 8.0,
     'L0_ffn_Wq': 48.543,
     'L0_ffn_keys_table': 42.517,
     'L0_ffn_values_table': 8.0,
     'L0_ffn_Wo': 8.0,
     'L1_ffn_w1': 7.461,
     'L1_ffn_w2': 5.352}
    for name, (base, spread) in spreads.items():
        noise = np.random.default_rng([zlib.crc32(name.encode()), seed]).standard_normal(out[name].shape)
        drawn = base * np.exp(spread * noise) if base else spread * noise
        out[name] = jnp.asarray(drawn.astype(out[name].dtype))
    for name, factor in factors.items():
        out[name] = (out[name] * factor).astype(out[name].dtype)
    return out
```

```python
from contextlib import ExitStack

import concourse.bass as bass
from concourse import mybir

F32 = mybir.dt.float32
F32R = mybir.dt.float32r
ALU = mybir.AluOpType
ACT = mybir.ActivationFunctionType
AX = mybir.AxisListType.X

P = 128
IMAGES, SEQ, D = 128, 64, 64
TOK = IMAGES * SEQ
BLK = 1024
HALF = BLK // 2
NBLK = TOK // BLK
TILES = BLK // P
IMG = BLK // SEQ
E = 128
TAPS = 5
HEADS = 8
NK = 64
KD = 32
TOPK = 16
UNITS = NBLK * HEADS
PAIRS = UNITS // 2
CHUNKS = 32
PER_Q = 8
QUARTERS = CHUNKS // PER_Q
BIG = 1e30
LOG_TINY = 87.3
SHIFT = LOG_TINY / 2
EPS = 1e-5
N = 128
EXP = 16
FF = 128
PI = 3.141592653589793
PI_SAFE = 3.1415925
CAND_BLOCKS = ((0, 1, 17), (1, 3, 8), (4, 13, 3))
NCAND = sum(na * nb for _, na, nb in CAND_BLOCKS)
LISTED = 24
ROWS = (("b2", D), ("bo", D), ("gate_b", EXP), ("ln_gamma", D), ("ln_beta", D))
NROW = sum(n for _, n in ROWS)
COLS = ("b1", "bd", "gamma", "beta", "rmean", "rvar", "A", "Dv")


def spread(ap, axis, n):
    u = ap.unsqueeze(axis)
    shape = list(u.shape)
    shape[axis] = n
    return u.broadcast_to(shape)


def hold(engine, passed):
    engine.sem_inc(passed, 1)


class Steps:

    def __init__(self, engine, sem, base=0):
        self.engine, self.sem, self.base, self.n = engine, sem, base, 0

    def did(self, instruction):
        instruction.then_inc(self.sem, 1)
        self.n += 1

    def settle(self):
        self.engine.wait_ge(self.sem, self.base + self.n)


class Norm:
    STEPS = 4

    def __init__(self, sb, name):
        self.mean = sb(name + "_mean", [P, TILES])
        self.centered = sb(name + "_centered", [P, TILES, D])
        self.square = sb(name + "_square", [P, TILES, D])
        self.sumsq = sb(name + "_sumsq", [P, TILES])
        self.std = sb(name + "_std", [P, TILES])
        self.rstd = sb(name + "_rstd", [P, TILES])

    def center(self, nc, s, z):
        v = nc.vector
        s.did(v.reduce_sum(self.mean[:], z, axis=AX))
        s.settle()
        s.did(v.scalar_tensor_tensor(self.centered[:], spread(self.mean[:], 2, D), -1.0 / D, z,
                                     ALU.mult, ALU.add))
        s.settle()
        s.did(v.tensor_tensor(self.square[:], self.centered[:], self.centered[:], ALU.mult))
        s.settle()
        return v.reduce_sum(self.sumsq[:], self.square[:], axis=AX)

    def root(self, nc, eps):
        return nc.scalar.activation(self.std[:], self.sumsq[:], ACT.Sqrt, bias=eps, scale=1.0 / D)

    def divide(self, nc, s, out):
        s.did(nc.vector.reciprocal(self.rstd[:], self.std[:]))
        s.settle()
        return nc.vector.tensor_tensor(out, self.centered[:], spread(self.rstd[:], 2, D), ALU.mult)


class Core:

    def __init__(self, nc, stack, inputs):
        self.nc, self.stack, self.inputs = nc, stack, inputs
        self.hT = self.sb("hT", [D, TOK])
        self.H = self.sb("H", [P, TOK // P, D])
        self.ident = self.sb("ident", [P, P])
        self.eps = self.sb("eps", [P, 1])
        self.passed = self.sem("passed")
        self.rowb = self.sb("rowb", [P, NROW])
        self.row, at = {}, 0
        for name, n in ROWS:
            self.row[name] = self.rowb[:, at:at + n]
            at += n

    def sb(self, name, shape, dt=F32, stack=None):
        return (stack or self.stack).enter_context(self.nc.sbuf_tensor(name, shape, dt))

    def ps(self, name, shape, stack):
        return stack.enter_context(self.nc.psum_tensor(name, shape, F32))

    def sem(self, name):
        return self.stack.enter_context(self.nc.semaphore(name))


def program(nc, inputs, out):
    with ExitStack() as stack:
        core = Core(nc, stack, inputs)
        mixer(core)
        memory(core)
        recurrent(core)
        experts(core, out)
    return nc


def mixer(core):
    nc, ins = core.nc, core.inputs
    hT, H, ident, eps, rowb, row = core.hT, core.H, core.ident, core.eps, core.rowb, core.row
    with ExitStack() as scope:
        def sb(name, shape, dt=F32):
            return core.sb(name, shape, dt, scope)

        tokw = sb("tokw", [E, 5])
        cols = sb("cols", [E, len(COLS)])
        col = {n: cols[:, i:i + 1] for i, n in enumerate(COLS)}
        bmcm = sb("bmcm", [E, 2, 8])
        taps = sb("taps", [E, TAPS])
        w1T = sb("w1T", [D, E])
        w2T = sb("w2T", [E, D])
        rows = sb("rows", [1, NROW])
        mean_w = sb("mean_w", [E, P])
        ones_row = sb("ones_row", [1, P])
        tokb = sb("tokb", [P, 5])
        w2state = sb("w2state", [E, D])
        w2skip = sb("w2skip", [E, D])
        bc = sb("bc", [E, 1])
        bcprod = sb("bcprod", [E, 8])
        bnstd = sb("bnstd", [E, 1])
        bninv = sb("bninv", [E, 1])
        bnscale = sb("bnscale", [E, 1])
        bnbias = sb("bnbias", [E, 1])
        bntmp = sb("bntmp", [E, 1])
        exp_a = sb("exp_a", [E, 1])
        decay = sb("decay", [E, IMG, SEQ])
        X = sb("X", [P, TILES, D, 4])
        h0 = sb("h0", [P, TILES, D])
        h0b = sb("h0b", [P, TILES, D])
        h0T = sb("h0T", [D, BLK])
        padded = sb("padded", [E, IMG, SEQ + TAPS - 1])
        conv = sb("conv", [E, IMG, SEQ])
        local = sb("local", [E, BLK])
        state = sb("state", [E, BLK])
        z = sb("z", [P, TILES, D])
        h1 = sb("h1", [P, TILES, D])
        norm = Norm(sb, "norm1")
        ps_small = core.ps("ps_small", [P, 512], scope)
        ps_T = core.ps("ps_T", [D, BLK], scope)
        ps_wide = core.ps("ps_wide", [E, BLK], scope)
        ps_out = core.ps("ps_out", [P, TILES, D], scope)

        weights_in = core.sem("weights_in")
        cleared = core.sem("cleared")
        consts = core.sem("consts")
        prep_step = core.sem("prep_step")
        means_ps = core.sem("means_ps")
        bn_root = core.sem("bn_root")
        decay_exp = core.sem("decay_exp")
        mix_step = core.sem("mix_step")
        x_in = core.sem("x_in")
        x_free = core.sem("x_free")
        h0_ready = core.sem("h0_ready")
        h0T_ps = core.sem("h0T_ps")
        h0T_ready = core.sem("h0T_ready")
        wide_ps = core.sem("wide_ps")
        gated = core.sem("gated")
        conv_ready = core.sem("conv_ready")
        local_ready = core.sem("local_ready")
        state_ready = core.sem("state_ready")
        out_ps = core.sem("out_ps")
        squares1 = core.sem("squares1")
        root1 = core.sem("root1")
        h1_ready = core.sem("h1_ready")
        h1T_ps = core.sem("h1T_ps")
        h1_stored = core.sem("h1_stored")

        LOADS = 7
        CLEARS = 5
        with nc.Block() as block:
            @block.sync
            def _(sp):
                for dst, name in ((tokw, "tokw"), (cols, "cols"), (bmcm, "bmcm"), (taps, "taps"),
                                  (w1T, "w1T"), (w2T, "w2T"), (rows, "rows")):
                    sp.dma_start(dst[:], ins[name]).then_inc(weights_in, 16)

            @block.gpsimd
            def _(pool):
                for t, value in ((ident, 0.0), (decay, 0.0), (padded, 0.0), (mean_w, 1.0 / E),
                                 (ones_row, 1.0)):
                    pool.memset(t[:], value).then_inc(cleared, 1)
                pool.memset(eps[:], EPS).then_inc(consts, 1)
                pool.wait_ge(cleared, CLEARS)
                pool.affine_select(out=ident[:], in_=ident[:], compare_op=ALU.not_equal, fill=1.0,
                                   base=0, pattern=[[-1, P]], channel_multiplier=1).then_inc(consts, 1)

            @block.tensor
            def _(pe):
                pe.wait_ge(weights_in, 16 * LOADS)
                pe.wait_ge(cleared, CLEARS)
                nc.tensor.matmul(ps_small[:, 0:5], mean_w[:], tokw[:], start=True, stop=True)
                nc.tensor.matmul(ps_small[:, 8:8 + NROW], ones_row[:], rows[:],
                                 start=True, stop=True).then_inc(means_ps, 1)

            @block.scalar
            def _(act):
                act.wait_ge(weights_in, 16 * LOADS)
                nc.scalar.activation(exp_a[:], col["A"], ACT.Exp).then_inc(decay_exp, 1)
                act.wait_ge(consts, 2)
                nc.scalar.activation(bnstd[:], col["rvar"], ACT.Sqrt, bias=eps[:, 0:1]).then_inc(bn_root, 1)

            @block.vector
            def _(dve):
                v = nc.vector
                s = Steps(dve, prep_step)
                dve.wait_ge(weights_in, 16 * LOADS)
                s.did(v.tensor_tensor(bcprod[:], bmcm[:, 0], bmcm[:, 1], ALU.mult))
                s.did(v.tensor_scalar(w2skip[:], w2T[:], col["Dv"], None, ALU.mult))
                s.settle()
                s.did(v.reduce_sum(bc[:], bcprod[:], axis=AX))
                s.settle()
                s.did(v.tensor_scalar(w2state[:], w2T[:], bc[:, 0:1], None, ALU.mult))
                dve.wait_ge(bn_root, 1)
                s.did(v.reciprocal(bninv[:], bnstd[:]))
                s.did(v.tensor_tensor(bntmp[:], col["bd"], col["rmean"], ALU.subtract))
                s.settle()
                s.did(v.tensor_tensor(bnscale[:], bninv[:], col["gamma"], ALU.mult))
                s.settle()
                s.did(v.scalar_tensor_tensor(bnbias[:], bntmp[:], bnscale[:, 0:1], col["beta"],
                                             ALU.mult, ALU.add))
                dve.wait_ge(decay_exp, 1)
                dve.wait_ge(cleared, CLEARS)
                s.did(v.tensor_scalar(decay[:, :, 1:SEQ], decay[:, :, 1:SEQ], exp_a[:, 0:1], None, ALU.add))
                dve.wait_ge(means_ps, 1)
                s.did(v.tensor_copy(tokb[:], ps_small[:, 0:5]))
                s.did(v.tensor_copy(rowb[:], ps_small[:, 8:8 + NROW]))
                s.settle()

        VEC = 3 + (TAPS - 1) + 1 + Norm.STEPS
        with nc.Block() as block:
            @block.sync
            def _(sp):
                with sp.Fori(0, NBLK) as b:
                    sp.wait_ge(x_free, b + 1)
                    sp.dma_start(X[:].rearrange("p t j f -> p t (j f)"),
                                 ins["x"][:, bass.ds(b * TILES, TILES), :]).then_inc(x_in, 16)

            @block.tensor
            def _(pe):
                with pe.Fori(0, NBLK) as b:
                    pe.wait_ge(h0_ready, b + 1)
                    hold(pe, core.passed)
                    for t in range(TILES):
                        last = nc.tensor.transpose(ps_T[:, t * P:(t + 1) * P], h0[:, t, :], ident[:])
                    last.then_inc(h0T_ps, 1)
                    pe.wait_ge(h0T_ready, b + 1)
                    for c in range(2):
                        cc = slice(c * HALF, (c + 1) * HALF)
                        last = nc.tensor.matmul(ps_wide[:, cc], w1T[:], h0T[:, cc], start=True, stop=True)
                    last.then_inc(wide_ps, 1)
                    pe.wait_ge(state_ready, b + 1)
                    for t in range(TILES):
                        tt = slice(t * P, (t + 1) * P)
                        nc.tensor.matmul(ps_out[:, t, :], state[:, tt], w2state[:], start=True, stop=False)
                        last = nc.tensor.matmul(ps_out[:, t, :], local[:, tt], w2skip[:],
                                                start=False, stop=True)
                    last.then_inc(out_ps, 1)
                    pe.wait_ge(h1_ready, b + 1)
                    hold(pe, core.passed)
                    for t in range(TILES):
                        last = nc.tensor.transpose(ps_T[:, t * P:(t + 1) * P], h1[:, t, :], ident[:])
                    last.then_inc(h1T_ps, 1)

            @block.scalar
            def _(act):
                with act.Fori(0, NBLK) as b:
                    act.wait_ge(h0T_ps, b + 1)
                    nc.scalar.copy(h0T[:], ps_T[:]).then_inc(h0T_ready, 1)
                    act.wait_ge(wide_ps, b + 1)
                    nc.scalar.activation(padded[:, :, 2:2 + SEQ],
                                         ps_wide[:].rearrange("p (i s) -> p i s", s=SEQ),
                                         ACT.Silu, bias=col["b1"]).then_inc(gated, 1)
                    act.wait_ge(conv_ready, b + 1)
                    nc.scalar.activation(local[:], conv[:].rearrange("p i s -> p (i s)"), ACT.Silu,
                                         bias=bnbias[:, 0:1], scale=bnscale[:, 0:1]).then_inc(local_ready, 1)
                    act.wait_ge(squares1, b + 1)
                    norm.root(nc, eps[:, 0:1]).then_inc(root1, 1)
                    act.wait_ge(h1T_ps, b + 1)
                    nc.scalar.copy(hT[:, bass.ds(b * BLK, BLK)], ps_T[:]).then_inc(h1_stored, 1)

            @block.gpsimd
            def _(pool):
                with pool.Fori(0, NBLK) as b:
                    pool.wait_ge(h1_ready, b + 1)
                    hold(pool, core.passed)
                    pool.tensor_copy(H[:, bass.ds(b * TILES, TILES), :], h1[:]).then_inc(h1_stored, 1)

            @block.vector
            def _(dve):
                v = nc.vector
                dve.sem_inc(x_free, 1)
                with dve.Fori(0, NBLK) as b:
                    s = Steps(dve, mix_step, b * VEC)
                    dve.wait_ge(x_in, 16 * (b + 1))
                    s.did(v.tensor_scalar(h0[:], X[:, :, :, 0], tokb[:, 0:1], tokb[:, 4:5], ALU.mult, ALU.add))
                    for f in (1, 2):
                        s.settle()
                        s.did(v.scalar_tensor_tensor(h0[:], X[:, :, :, f], tokb[:, f:f + 1], h0[:],
                                                     ALU.mult, ALU.add))
                    s.settle()
                    v.scalar_tensor_tensor(h0[:], X[:, :, :, 3], tokb[:, 3:4], h0[:],
                                           ALU.mult, ALU.add).then_inc(h0_ready, 1)
                    dve.wait_ge(h0_ready, b + 1)
                    v.tensor_tensor(h0b[:], h0[:], spread(row["b2"], 1, TILES), ALU.add).then_inc(x_free, 1)
                    dve.wait_ge(gated, b + 1)
                    s.did(v.tensor_scalar(conv[:], padded[:, :, 0:SEQ], taps[:, 0:1], None, ALU.mult))
                    for k in range(1, TAPS - 1):
                        s.settle()
                        s.did(v.scalar_tensor_tensor(conv[:], padded[:, :, k:k + SEQ], taps[:, k:k + 1],
                                                     conv[:], ALU.mult, ALU.add))
                    s.settle()
                    v.scalar_tensor_tensor(conv[:], padded[:, :, TAPS - 1:TAPS - 1 + SEQ],
                                           taps[:, TAPS - 1:TAPS], conv[:],
                                           ALU.mult, ALU.add).then_inc(conv_ready, 1)
                    dve.wait_ge(local_ready, b + 1)
                    v.tensor_tensor_scan(state[:], decay[:].rearrange("p i s -> p (i s)"), local[:], 0.0,
                                         ALU.mult, ALU.add).then_inc(state_ready, 1)
                    dve.wait_ge(out_ps, b + 1)
                    s.did(v.tensor_tensor(z[:], ps_out[:], h0b[:], ALU.add))
                    s.settle()
                    norm.center(nc, s, z[:]).then_inc(squares1, 1)
                    dve.wait_ge(root1, b + 1)
                    norm.divide(nc, s, h1[:]).then_inc(h1_ready, 1)
                    dve.wait_ge(h1_stored, 2 * (b + 1))
                    assert s.n == VEC, s.n


def memory(core):
    nc, ins = core.nc, core.inputs
    hT, H, ident = core.hT, core.H, core.ident
    with ExitStack() as scope:
        def sb(name, shape, dt=F32):
            return core.sb(name, shape, dt, scope)

        wqp = sb("wqp", [KD, 2 * HEADS, D])
        keys = sb("keys", [KD, 2 * HEADS, NK])
        score_w = sb("score_w", [D, HEADS, 2 * NK])
        wq_all = sb("wq_all", [D, HEADS * D])
        lower = sb("lower", [P, P])
        causal2 = sb("causal2", [P, 2, SEQ])
        causal = sb("causal", [P, SEQ])
        pick32 = sb("pick32", [P, PER_Q, 4, 32])
        pick = sb("pick", [P, PER_Q, P], F32R)
        hTb = sb("hTb", [D, BLK])
        score_wh = sb("score_wh", [D, 2 * NK])
        wqh = sb("wqh", [D, D])
        woh = [sb(f"woh{i}", [P, D]) for i in range(2)]
        sims = sb("sims", [P, TILES, 2 * NK])
        rest = [sb(f"rest{i}", [P, 2, 2, NK]) for i in range(2)]
        listed = sb("listed", [P, 2, TILES, LISTED])
        cand = sb("cand", [P, TILES, NCAND])
        cand_rest = [sb(f"cand_rest{i}", [P, 4, NCAND]) for i in range(2)]
        final = sb("final", [P, TILES, LISTED])
        mid = sb("mid", [P, TILES])
        neg_top = sb("neg_top", [P, TILES])
        neg_thr = sb("neg_thr", [P, TILES])
        over = sb("over", [P, TILES, TOPK])
        over_exp = sb("over_exp", [P, TILES, TOPK])
        kept = sb("kept", [P, TILES, TOPK])
        den = sb("den", [P, TILES])
        rden = [sb(f"rden{i}", [P, TILES]) for i in range(2)]
        diag = sb("diag", [P, TILES, P])
        hi = sb("hi", [P, BLK], F32R)
        lo = sb("lo", [P, BLK], F32R)
        scores = [sb(f"scores{i}", [P, QUARTERS, BLK], F32R) for i in range(2)]
        qT = [sb(f"qT{i}", [D, BLK]) for i in range(2)]
        table = sb("table", [P, QUARTERS, PER_Q, 2 * D])
        expo = [sb(f"expo{i}", [P, BLK]) for i in range(2)]
        weight = [sb(f"weight{i}", [P, BLK]) for i in range(2)]
        accS = sb("accS", [P, BLK])
        kv = sb("kv", [P, 2, TILES, D])
        kT = sb("kT", [D, BLK])
        masked = sb("masked", [P, TILES, SEQ])
        top1 = sb("top1", [P, TILES])
        shifted = sb("shifted", [P, TILES, SEQ])
        probs = sb("probs", [P, TILES, P])
        probsT = sb("probsT", [P, TILES, P])
        psumr = sb("psumr", [P, TILES])
        rsum = sb("rsum", [P, TILES])
        y = sb("y", [P, TILES, D])
        shift = sb("shift", [P, 1])

        psS = [core.ps(f"psS{i}", [P, BLK], scope) for i in range(2)]
        acc = core.ps("acc", [P, BLK], scope)
        side = core.ps("side", [P, BLK], scope)

        names = """keys_in masks_cleared masks_made masks_final pick_made score_w_ps mem_prep
            staged wo_in sims_ps sims_ready mem_step exp_in exp_done thr_ready diag_ready q_ps q_ready
            scores_ps hi_ready lo_ready s_ready e_ready w_ready w_used acc_copied kv_ps kv_ready kT_ps
            kT_ready logits_ps logits_ready probs_ready probsT_ps probsT_ready y_ps y_ready y_added"""
        q = {n: core.sem(n) for n in names.split()}
        scores_in = [core.sem(f"scores_in{i}") for i in range(2)]
        table_in = [core.sem(f"table_in{i}") for i in range(QUARTERS)]

        with nc.Block() as block:
            @block.sync
            def _(sp):
                sp.dma_start(wqp[:], ins["wqpkT"]).then_inc(q["keys_in"], 16)
                sp.dma_start(keys[:], ins["keysT"]).then_inc(q["keys_in"], 16)
                sp.dma_start(wq_all[:], ins["wq"]).then_inc(q["keys_in"], 16)
                sp.wait_ge(q["keys_in"], 48)

            @block.gpsimd
            def _(pool):
                pool.memset(lower[:, 0:NK], 0.0).then_inc(q["masks_cleared"], 1)
                pool.memset(lower[:, NK:P], 1.0).then_inc(q["masks_cleared"], 1)
                pool.memset(causal2[:], 0.0).then_inc(q["masks_cleared"], 1)
                pool.memset(pick32[:], 0.0).then_inc(q["masks_cleared"], 1)
                pool.memset(probs[:], 0.0).then_inc(q["masks_cleared"], 1)
                pool.memset(shift[:], -SHIFT).then_inc(q["masks_cleared"], 1)
                pool.wait_ge(q["masks_cleared"], 6)
                pool.affine_select(out=causal2[:], in_=causal2[:], compare_op=ALU.is_ge, fill=-BIG, base=0,
                                   pattern=[[-SEQ, 2], [-1, SEQ]], channel_multiplier=1
                                   ).then_inc(q["masks_made"], 1)
                for n, (base, pattern) in enumerate((
                        (0, [[0, PER_Q], [0, 4], [-1, 32]]), (-32, [[0, PER_Q], [0, 4], [-1, 32]]),
                        (-64, [[-4, PER_Q], [-1, 4], [0, 32]]), (-96, [[-4, PER_Q], [-1, 4], [0, 32]]))):
                    pool.affine_select(out=pick32[:], in_=pick32[:], compare_op=ALU.not_equal, fill=1.0,
                                       base=base, pattern=pattern, channel_multiplier=1
                                       ).then_inc(q["pick_made"], 1)
                    pool.wait_ge(q["pick_made"], n + 1)

            @block.tensor
            def _(pe):
                pe.wait_ge(q["keys_in"], 48)
                for h in range(HEADS):
                    for p in range(2):
                        last = nc.tensor.matmul(side[0:D, (h * 2 + p) * NK:(h * 2 + p + 1) * NK],
                                                wqp[:, p * HEADS + h, :], keys[:, p * HEADS + h, :],
                                                start=True, stop=True)
                last.then_inc(q["score_w_ps"], 1)

            @block.vector
            def _(dve):
                s = Steps(dve, q["mem_prep"])
                dve.wait_ge(q["score_w_ps"], 1)
                s.did(nc.vector.tensor_copy(score_w[:].rearrange("p h k -> p (h k)"), side[0:D, :]))
                dve.wait_ge(q["masks_made"], 1)
                for i in range(2):
                    hp = slice(i * SEQ, (i + 1) * SEQ)
                    s.did(nc.vector.tensor_copy(causal[hp, :], causal2[hp, i, :]))
                dve.wait_ge(q["pick_made"], 4)
                s.did(nc.vector.tensor_copy(pick[:].rearrange("p m (a b) -> p m a b", a=4), pick32[:]))
                s.settle()

        CREDIT = CHUNKS
        J_SIMS, J_KV, J_KT, J_LOGITS, J_PROBST, J_Y, J_Q, J_SCORES = 1, 3, 6, 8, 13, 16, 18, 28
        LIST_STEPS, FINAL_STEPS = 20, 10
        SELECT_STEPS = LIST_STEPS + 1 + FINAL_STEPS + 3
        PREP_COUNT = 4 * 5 * 4 + len(CAND_BLOCKS) + 2 * 5 * 4 + 2 + 2
        ATTN_COUNT = 2 + 2 + 0
        first, last_slot = J_SIMS + 1, J_SCORES - 2
        select_at = [min(max(0, -(-(k - first) * SELECT_STEPS // (last_slot - first))), SELECT_STEPS)
                     for k in range(CHUNKS + 1)]

        with nc.Block() as block:
            @block.sync
            def _(sp):
                with sp.Fori(0, NBLK) as b:
                    with sp.Fori(0, HEADS // 2) as hp:
                        for par in range(2):
                            v = b * HEADS + hp * 2 + par
                            head = hp * 2 + par
                            sp.wait_ge(q["scores_ps"], v + 1)
                            sp.dma_start(hTb[:], hT[:, bass.ds(b * BLK, BLK)]).then_inc(q["staged"], 16)
                            sp.dma_start(score_wh[:].unsqueeze(1), score_w[:, bass.ds(head, 1), :]
                                         ).then_inc(q["staged"], 16)
                            sp.dma_start(wqh[:], wq_all[:, bass.ds(head * D, D)]).then_inc(q["staged"], 16)
                            for c in range(QUARTERS):
                                if c == QUARTERS - 1:
                                    sp.wait_ge(q["hi_ready"], v + 1)
                                    sp.wait_ge(q["lo_ready"], v + 1)
                                    for part, src in enumerate((hi, lo)):
                                        for a in range(2):
                                            sp.dma_start(
                                                scores[par][32 * part:32 * part + 32, 2 * a:2 * a + 2, :].bitcast(F32),
                                                spread(src[32 * a:32 * a + 32, :].bitcast(F32), 1, 2)
                                            ).then_inc(scores_in[par], 16)
                                            at = 64 + 32 * part
                                            sp.dma_start(
                                                scores[par][at:at + 32, a:a + 3:2, :].bitcast(F32),
                                                spread(src[64 + 32 * a:96 + 32 * a, :].bitcast(F32), 1, 2)
                                            ).then_inc(scores_in[par], 16)
                                sp.wait_ge(q["w_used"], v * CHUNKS + (c + 1) * PER_Q)
                                sp.dma_start(table[:, c].rearrange("p m d -> p (m d)").unsqueeze(1),
                                             ins["table"][:, bass.ds(head * QUARTERS + c, 1), :]
                                             ).then_inc(table_in[c], 16)
                                if c == 0:
                                    sp.dma_start(woh[par][D:P, :].unsqueeze(1),
                                                 ins["wo"][:, bass.ds(head, 1), :]).then_inc(q["wo_in"], 16)

            @block.gpsimd
            def _(pool):
                def make_diag(v):
                    pool.wait_ge(q["thr_ready"], v + 1)
                    pool.tensor_tensor(diag[:], spread(ident[:], 1, TILES), spread(neg_thr[:], 2, P),
                                       ALU.mult).then_inc(q["diag_ready"], 1)

                def add_output(b, w):
                    pool.wait_ge(q["y_ready"], w + 1)
                    pool.tensor_tensor(H[:, bass.ds(b * TILES, TILES), :], H[:, bass.ds(b * TILES, TILES), :],
                                       y[:], ALU.add).then_inc(q["y_added"], 1)
                    pool.wait_ge(q["y_added"], w + 1)

                make_diag(0)
                make_diag(1)
                with pool.Fori(0, NBLK - 1) as b:
                    with pool.Fori(0, HEADS) as h:
                        add_output(b, b * HEADS + h)
                        make_diag(b * HEADS + h + 2)
                with pool.Fori(0, HEADS - 2) as h:
                    add_output(NBLK - 1, h + (NBLK - 1) * HEADS)
                    make_diag(h + (NBLK - 1) * HEADS + 2)
                for h in range(HEADS - 2, HEADS):
                    add_output(NBLK - 1, (NBLK - 1) * HEADS + h)

            @block.tensor
            def _(pe):
                mm = nc.tensor.matmul

                def similarities(v):
                    pe.wait_ge(q["staged"], 48 * (v + 1))
                    if not (isinstance(v, int) and v == 0):
                        pe.wait_ge(q["lo_ready"], v)
                    for t in range(TILES):
                        last = mm(side[:, t * P:(t + 1) * P], hTb[:, t * P:(t + 1) * P], score_wh[:],
                                  start=True, stop=True)
                    last.then_inc(q["sims_ps"], 1)

                def queries(v):
                    pe.wait_ge(q["sims_ready"], v + 1)
                    if not (isinstance(v, int) and v < 2):
                        pe.wait_ge(q["y_ready"], v - 1)
                    hold(pe, core.passed)
                    for c in range(2):
                        cc = slice(c * HALF, (c + 1) * HALF)
                        last = mm(side[0:D, cc], wqh[:], hTb[:, cc], start=True, stop=True)
                    last.then_inc(q["q_ps"], 1)

                def thresholded(v):
                    pe.wait_ge(q["q_ready"], v + 1)
                    pe.wait_ge(q["diag_ready"], v + 1)
                    for c in range(2):
                        cc = slice(c * HALF, (c + 1) * HALF)
                        mm(side[:, cc], score_wh[:], hTb[:, cc], start=True, stop=False)
                        for t in range(4 * c, 4 * c + 4):
                            last = mm(side[:, t * P:(t + 1) * P], lower[:], diag[:, t, :],
                                      start=False, stop=t == 4 * c + 3)
                    last.then_inc(q["scores_ps"], 1)

                def gathered(w, par):
                    pe.wait_ge(q["acc_copied"], w + 1)
                    pe.wait_ge(q["wo_in"], 16 * (w + 1))
                    if not (isinstance(w, int) and w >= UNITS - 2):
                        pe.wait_ge(q["sims_ready"], w + 3)
                    for t in range(TILES):
                        tt = slice(t * P, (t + 1) * P)
                        mm(side[:, HALF + t * D:HALF + (t + 1) * D], accS[D:P, tt], woh[par][D:P, :],
                           start=True, stop=True)
                        last = nc.tensor.transpose(side[:, t * D:(t + 1) * D], accS[0:D, tt], ident[0:D, 0:D])
                    last.then_inc(q["kv_ps"], 1)

                def keys_back(w):
                    pe.wait_ge(q["kv_ready"], w + 1)
                    hold(pe, core.passed)
                    for t in range(TILES):
                        last = nc.tensor.transpose(side[0:D, t * P:(t + 1) * P], kv[:, 0, t, :], ident[:])
                    last.then_inc(q["kT_ps"], 1)

                def logits(w, par):
                    pe.wait_ge(q["kT_ready"], w + 1)
                    hold(pe, core.passed)
                    for t in range(TILES):
                        for i in range(2):
                            at = slice(t * P + i * SEQ, t * P + (i + 1) * SEQ)
                            last = mm(side[i * SEQ:(i + 1) * SEQ, t * SEQ:(t + 1) * SEQ],
                                      qT[par][:, at], kT[:, at], start=True, stop=True)
                    last.then_inc(q["logits_ps"], 1)

                def probs_transposed(w):
                    pe.wait_ge(q["probs_ready"], 2 * (w + 1))
                    for t in range(TILES):
                        last = nc.tensor.transpose(side[:, t * P:(t + 1) * P], probs[:, t, :], ident[:])
                    last.then_inc(q["probsT_ps"], 1)

                def attend(w):
                    pe.wait_ge(q["probsT_ready"], w + 1)
                    for t in range(TILES):
                        last = mm(side[:, t * D:(t + 1) * D], probsT[:, t, :], kv[:, 1, t, :],
                                  start=True, stop=True)
                    last.then_inc(q["y_ps"], 1)

                def product(u, k, begins):
                    pe.wait_ge(q["w_ready"], u * CHUNKS + (k + 1))
                    if k % PER_Q == 0:
                        pe.wait_ge(table_in[k // PER_Q], 16 * (u + 1))
                    if k == 0 and not begins:
                        pe.wait_ge(q["acc_copied"], u)
                    for c in range(2):
                        cc = slice(c * HALF, (c + 1) * HALF)
                        last = mm(acc[:, cc], table[:, k // PER_Q, k % PER_Q, :], weight[k % 2][:, cc],
                                  start=k == 0, stop=k == CHUNKS - 1)
                    last.then_inc(q["w_used"], 1)

                def unit(u, par, i, begins=False, attention=True, prepare=True):
                    for k in range(CHUNKS):
                        if k == 0:
                            pe.wait_ge(scores_in[par], 16 * 8 * (i + 1))
                        if not (begins and k < 2):
                            pe.wait_ge(q["w_ready"], u * CHUNKS + (k - 1))
                        for c in range(2):
                            cc = slice(c * HALF, (c + 1) * HALF)
                            last = mm(psS[k % 2][:, cc], pick[:, k % PER_Q, :],
                                      scores[par][:, k // PER_Q, cc], start=True, stop=True)
                        last.then_inc(q["s_ready"], 1)
                        if k > 0:
                            product(u, k - 1, begins)
                        elif not begins:
                            product(u - 1, CHUNKS - 1, False)
                        if k == J_SIMS and prepare:
                            similarities(u + 1)
                        if attention:
                            if k == J_KV:
                                gathered(u - 1, 1 - par)
                            if k == J_KT:
                                keys_back(u - 1)
                            if k == J_LOGITS:
                                logits(u - 1, 1 - par)
                            if k == J_PROBST:
                                probs_transposed(u - 1)
                            if k == J_Y:
                                attend(u - 1)
                        if k == J_Q and prepare:
                            queries(u + 1)
                        if k == J_SCORES and prepare:
                            thresholded(u + 1)

                pe.sem_inc(q["w_used"], CREDIT)
                pe.sem_inc(q["scores_ps"], 1)
                similarities(0)
                queries(0)
                thresholded(0)
                unit(0, 0, 0, begins=True, attention=False)
                unit(1, 1, 0)
                with pe.Fori(1, PAIRS - 1) as i:
                    for par in range(2):
                        unit(i * 2 + par, par, i)
                unit(UNITS - 2, 0, PAIRS - 1)
                unit(UNITS - 1, 1, PAIRS - 1, prepare=False)
                product(UNITS - 1, CHUNKS - 1, False)
                gathered(UNITS - 1, 1)
                keys_back(UNITS - 1)
                logits(UNITS - 1, 1)
                probs_transposed(UNITS - 1)
                attend(UNITS - 1)

            @block.scalar
            def _(act):
                a = nc.scalar

                def copy_sims(v):
                    act.wait_ge(q["sims_ps"], v + 1)
                    a.copy(sims[:].rearrange("p t k -> p (t k)"), side[:]).then_inc(q["sims_ready"], 1)

                def exp_over(v):
                    act.wait_ge(q["exp_in"], v + 1)
                    a.activation(over_exp[:], over[:], ACT.Exp, bias=shift[:, 0:1]).then_inc(q["exp_done"], 1)

                def copy_queries(v, par):
                    act.wait_ge(q["q_ps"], v + 1)
                    a.activation(qT[par][:], side[0:D, :], ACT.Copy, scale=float(D) ** -0.5
                                 ).then_inc(q["q_ready"], 1)

                def high_parts(v, i_before, par_before):
                    act.wait_ge(q["scores_ps"], v + 2)
                    if i_before is not None:
                        act.wait_ge(scores_in[par_before], 16 * 8 * (i_before + 1))
                    a.copy(hi[:], side[:]).then_inc(q["hi_ready"], 1)

                def copy_acc(w):
                    act.wait_ge(q["w_used"], CREDIT + CHUNKS * (w + 1))
                    a.copy(accS[:], acc[:]).then_inc(q["acc_copied"], 1)

                def copy_kT(w):
                    act.wait_ge(q["kT_ps"], w + 1)
                    a.copy(kT[:], side[0:D, :]).then_inc(q["kT_ready"], 1)

                def exp_probs(w):
                    act.wait_ge(q["logits_ready"], w + 1)
                    for i in range(2):
                        at = slice(i * SEQ, (i + 1) * SEQ)
                        a.activation(probs[at, :, at], shifted[at], ACT.Exp).then_inc(q["probs_ready"], 1)

                def copy_probsT(w):
                    act.wait_ge(q["probsT_ps"], w + 1)
                    a.copy(probsT[:].rearrange("p t k -> p (t k)"), side[:]).then_inc(q["probsT_ready"], 1)

                def unit(u, par, i, begins=False, attention=True, prepare=True):
                    for k in range(CHUNKS):
                        act.wait_ge(q["s_ready"], u * CHUNKS + (k + 1))
                        if not (begins and k < 2):
                            act.wait_ge(q["w_ready"], u * CHUNKS + (k - 1))
                        a.activation(expo[k % 2][:], psS[k % 2][:], ACT.Exp, bias=shift[:, 0:1]
                                     ).then_inc(q["e_ready"], 1)
                        if k == 1 and not begins:
                            copy_acc(u - 1)
                        if k == J_SIMS + 1 and prepare:
                            copy_sims(u + 1)
                        if attention:
                            if k == J_KT + 1:
                                copy_kT(u - 1)
                            if k == J_LOGITS + 2:
                                exp_probs(u - 1)
                            if k == J_PROBST + 1:
                                copy_probsT(u - 1)
                        if k == J_Q + 1 and prepare:
                            copy_queries(u + 1, 1 - par)
                        if k == J_SCORES + 1 and prepare:
                            high_parts(u + 1, i, par)
                        if k == J_SCORES + 2 and prepare:
                            exp_over(u + 1)

                copy_sims(0)
                copy_queries(0, 0)
                high_parts(0, None, None)
                exp_over(0)
                unit(0, 0, 0, begins=True, attention=False)
                unit(1, 1, 0)
                with act.Fori(1, PAIRS - 1) as i:
                    for par in range(2):
                        unit(i * 2 + par, par, i)
                unit(UNITS - 2, 0, PAIRS - 1)
                unit(UNITS - 1, 1, PAIRS - 1, prepare=False)
                copy_acc(UNITS - 1)
                copy_kT(UNITS - 1)
                exp_probs(UNITS - 1)
                copy_probsT(UNITS - 1)

            @block.vector
            def _(dve):
                v_ = nc.vector

                def sort_stage(s, stage, items):
                    for out, source, rest_a, rest_b in items:
                        if stage == 0:
                            s.did(v_.max(out[:, 0:8], source))
                        elif stage == 1:
                            s.did(v_.match_replace(rest_a, out[:, 0:8], source, -BIG))
                        elif stage == 2:
                            s.did(v_.max(out[:, 8:16], rest_a))
                        elif stage == 3:
                            s.did(v_.match_replace(rest_b, out[:, 8:16], rest_a, -BIG))
                        else:
                            s.did(v_.max(out[:, 16:24], rest_b))

                def select(s, n, v, par):
                    if n == 0:
                        dve.wait_ge(q["sims_ready"], v + 1)
                    elif n != SELECT_STEPS - 2:
                        s.settle()
                    if n != LIST_STEPS and n < SELECT_STEPS - 3:
                        hold(dve, core.passed)
                    if n < LIST_STEPS:
                        group, stage = divmod(n, 5)
                        sort_stage(s, stage, [
                            (listed[:, p, t, :], sims[:, t, p * NK:(p + 1) * NK],
                             rest[0][:, t % 2, p, :], rest[1][:, t % 2, p, :])
                            for t in (2 * group, 2 * group + 1) for p in range(2)])
                    elif n == LIST_STEPS:
                        at = 0
                        for a0, na, nb in CAND_BLOCKS:
                            block_out = cand[:, :, at:at + na * nb].rearrange("p t (a b) -> p t a b", a=na)
                            s.did(v_.tensor_tensor(block_out, spread(listed[:, 0, :, a0:a0 + na], 3, nb),
                                                   spread(listed[:, 1, :, 0:nb], 2, na), ALU.add))
                            at += na * nb
                    elif n <= LIST_STEPS + FINAL_STEPS:
                        group, stage = divmod(n - LIST_STEPS - 1, 5)
                        sort_stage(s, stage, [
                            (final[:, t, :], cand[:, t, :], cand_rest[0][:, t % 4, :], cand_rest[1][:, t % 4, :])
                            for t in range(4 * group, 4 * group + 4)])
                    elif n == SELECT_STEPS - 3:
                        s.did(v_.tensor_tensor(mid[:], final[:, :, TOPK - 1], final[:, :, TOPK], ALU.add))
                        s.did(v_.tensor_scalar(neg_top[:], final[:, :, 0], -1.0, LOG_TINY, ALU.mult, ALU.add))
                        s.settle()
                        v_.scalar_tensor_tensor(neg_thr[:], mid[:], -0.5, neg_top[:], ALU.mult, ALU.min
                                                ).then_inc(q["thr_ready"], 1)
                    elif n == SELECT_STEPS - 2:
                        dve.wait_ge(q["thr_ready"], v + 1)
                        v_.tensor_tensor(over[:], final[:, :, 0:TOPK], spread(neg_thr[:], 2, TOPK), ALU.add
                                         ).then_inc(q["exp_in"], 1)

                def denominators(s, v, par):
                    dve.wait_ge(q["exp_done"], v + 1)
                    s.did(v_.scalar_tensor_tensor(kept[:], over[:], 0.0, over_exp[:], ALU.is_ge, ALU.mult))
                    s.settle()
                    s.did(v_.reduce_sum(den[:], kept[:], axis=AX))
                    s.settle()
                    v_.reciprocal(rden[par][:], den[:])

                def low_parts(v):
                    dve.wait_ge(q["hi_ready"], v + 1)
                    v_.tensor_tensor(lo[:], side[:], hi[:].bitcast(F32), ALU.subtract).then_inc(q["lo_ready"], 1)

                def normalized(w, par):
                    dve.wait_ge(q["kv_ps"], w + 1)
                    v_.tensor_tensor(kv[:], side[:].rearrange("p (a t d) -> p a t d", a=2, t=TILES),
                                     spread(spread(rden[par][:], 2, D), 1, 2), ALU.mult
                                     ).then_inc(q["kv_ready"], 1)

                def softmax_in(s, w):
                    dve.wait_ge(q["logits_ps"], w + 1)
                    s.did(v_.tensor_tensor(masked[:], side[:, 0:HALF].rearrange("p (t k) -> p t k", t=TILES),
                                           spread(causal[:], 1, TILES), ALU.add))
                    s.settle()
                    s.did(v_.reduce_max(top1[:], masked[:], axis=AX))
                    s.settle()
                    v_.tensor_tensor(shifted[:], masked[:], spread(top1[:], 2, SEQ), ALU.subtract
                                     ).then_inc(q["logits_ready"], 1)

                def softmax_sum(s, w):
                    dve.wait_ge(q["probs_ready"], 2 * (w + 1))
                    s.did(v_.reduce_sum(psumr[:], probs[:], axis=AX))
                    s.settle()
                    s.did(v_.reciprocal(rsum[:], psumr[:]))

                def output(s, w):
                    dve.wait_ge(q["y_ps"], w + 1)
                    s.settle()
                    v_.tensor_tensor(y[:], side[:, 0:HALF].rearrange("p (t d) -> p t d", t=TILES),
                                     spread(rsum[:], 2, D), ALU.mult).then_inc(q["y_ready"], 1)

                def unit(s, u, par, begins=False, attention=True, prepare=True):
                    for k in range(CHUNKS):
                        dve.wait_ge(q["e_ready"], u * CHUNKS + (k + 1))
                        if not (begins and k < 2):
                            dve.wait_ge(q["w_used"], u * CHUNKS + (CREDIT + k - 1))
                        v_.scalar_tensor_tensor(weight[k % 2][:], psS[k % 2][:], 0.0, expo[k % 2][:],
                                                ALU.is_ge, ALU.mult).then_inc(q["w_ready"], 1)
                        if attention:
                            if k == J_KV + 1:
                                normalized(u - 1, 1 - par)
                            if k == J_LOGITS + 1:
                                softmax_in(s, u - 1)
                            if k == J_LOGITS + 4:
                                softmax_sum(s, u - 1)
                            if k == J_Y + 1:
                                output(s, u - 1)
                        if prepare:
                            for n in range(select_at[k], select_at[k + 1]):
                                select(s, n, u + 1, 1 - par)
                            if k == J_SCORES + 2:
                                low_parts(u + 1)
                            if k == J_SCORES + 3:
                                denominators(s, u + 1, 1 - par)

                COUNT = PREP_COUNT + ATTN_COUNT
                s = Steps(dve, q["mem_step"])
                for n in range(SELECT_STEPS):
                    select(s, n, 0, 0)
                low_parts(0)
                denominators(s, 0, 0)
                assert s.n == PREP_COUNT, s.n
                unit(s, 0, 0, begins=True, attention=False)
                unit(s, 1, 1)
                before = s.n
                assert before == 3 * PREP_COUNT + ATTN_COUNT, s.n
                with dve.Fori(1, PAIRS - 1) as i:
                    s = Steps(dve, q["mem_step"], i * (2 * COUNT) + (before - 2 * COUNT))
                    for par in range(2):
                        unit(s, i * 2 + par, par)
                    assert s.n == 2 * COUNT
                s = Steps(dve, q["mem_step"], before + (PAIRS - 2) * 2 * COUNT)
                unit(s, UNITS - 2, 0)
                unit(s, UNITS - 1, 1, prepare=False)
                normalized(UNITS - 1, 1)
                softmax_in(s, UNITS - 1)
                softmax_sum(s, UNITS - 1)
                dve.wait_ge(q["y_added"], UNITS - 1)
                output(s, UNITS - 1)


def recurrent(core):
    nc, ins = core.nc, core.inputs
    hT, H, ident, eps, row = core.hT, core.H, core.ident, core.eps, core.row
    with ExitStack() as scope:
        def sb(name, shape, dt=F32):
            return core.sb(name, shape, dt, scope)

        wiT = sb("wiT", [D, 2, N])
        bi = sb("bi", [N, 2])
        woT = sb("woT", [N, 2, D])
        plog = sb("plog", [N, 3])
        params = sb("params", [N, 3])
        wog = sb("wog", [N, 2, D])
        rate = sb("rate", [N, 1])
        decay = sb("decay_c", [N, IMG, SEQ])
        pos = sb("pos", [N, SEQ])
        angle = sb("angle", [N, SEQ])
        turns = sb("turns", [N, SEQ])
        red = sb("red", [N, SEQ])
        red2 = sb("red2", [N, SEQ])
        wrap = sb("wrap", [N, SEQ])
        cos = sb("cos", [N, SEQ])
        sin = sb("sin", [N, SEQ])
        z2 = sb("z2", [P, TILES, D])
        h2 = sb("h2", [P, TILES, D])
        h2b = sb("h2b", [P, TILES, D])
        h2T = sb("h2T", [D, BLK])
        ur = sb("ur", [N, IMG, SEQ])
        ui = sb("ui", [N, IMG, SEQ])
        vr = sb("vr", [N, IMG, SEQ])
        vi = sb("vi", [N, IMG, SEQ])
        t1 = sb("t1", [N, IMG, SEQ])
        t2 = sb("t2", [N, IMG, SEQ])
        yr = sb("yr", [N, IMG, SEQ])
        yi = sb("yi", [N, IMG, SEQ])
        xr = sb("xr", [N, IMG, SEQ])
        xi = sb("xi", [N, IMG, SEQ])
        z3 = sb("z3", [P, TILES, D])
        h3 = sb("h3", [P, TILES, D])
        norm2 = Norm(sb, "norm2")
        norm3 = Norm(sb, "norm3")
        ps_T = core.ps("ps_T2", [D, BLK], scope)
        ps_u = core.ps("ps_u", [N, 2, BLK], scope)
        ps_y = core.ps("ps_y", [P, TILES, D], scope)

        names = """rec_in rec_cleared rec_params rec_rate rec_trig rec_prep rec_angle rec_step z2_in
            squares2 root2 h2_ready h2T_ps h2T_ready u_ps u_ready v_pool rot_ready scan_ready x_pool
            x_ready y3_ps squares3 root3 h3_ready h3T_ps h3_stored"""
        q = {n: core.sem(n) for n in names.split()}

        with nc.Block() as block:
            @block.sync
            def _(sp):
                for dst, name in ((wiT, "wiT"), (bi, "bi"), (woT, "woT"), (plog, "plog")):
                    sp.dma_start(dst[:], ins[name]).then_inc(q["rec_in"], 16)

            @block.gpsimd
            def _(pool):
                pool.memset(decay[:], 0.0).then_inc(q["rec_cleared"], 1)
                pool.iota(pos[:], pattern=[[1, SEQ]], base=0, channel_multiplier=0,
                          allow_small_or_imprecise_dtypes=True).then_inc(q["rec_cleared"], 1)

            @block.scalar
            def _(act):
                act.wait_ge(q["rec_in"], 64)
                nc.scalar.activation(params[:], plog[:], ACT.Exp).then_inc(q["rec_params"], 1)
                act.wait_ge(q["rec_params"], 1)
                nc.scalar.activation(rate[:], params[:, 0:1], ACT.Exp, scale=-1.0).then_inc(q["rec_rate"], 1)
                act.wait_ge(q["rec_angle"], 1)
                nc.scalar.activation(sin[:], red[:], ACT.Sin).then_inc(q["rec_trig"], 1)
                nc.scalar.activation(cos[:], wrap[:], ACT.Sin).then_inc(q["rec_trig"], 1)
                act.wait_ge(q["rec_trig"], 2)

            @block.vector
            def _(dve):
                v = nc.vector
                s = Steps(dve, q["rec_prep"])
                dve.wait_ge(q["rec_cleared"], 2)
                dve.wait_ge(q["rec_params"], 1)
                s.did(v.tensor_scalar(angle[:], pos[:], params[:, 1:2], None, ALU.mult))
                s.did(v.tensor_scalar(wog[:].rearrange("p a d -> p (a d)"),
                                      woT[:].rearrange("p a d -> p (a d)"), params[:, 2:3], None, ALU.mult))
                s.settle()
                ROUND = 12582912.0
                s.did(v.tensor_scalar(turns[:], angle[:], 1.0 / (2 * PI), ROUND, ALU.mult, ALU.add))
                s.settle()
                s.did(v.tensor_scalar(turns[:], turns[:], -ROUND, None, ALU.add))
                s.settle()
                parts = (6.28125, 0.0019340515136718750, 2 * PI - 6.28125 - 0.0019340515136718750)
                src, dst = angle, red
                for part in parts:
                    s.did(v.scalar_tensor_tensor(dst[:], turns[:], -part, src[:], ALU.mult, ALU.add))
                    s.settle()
                    src, dst = dst, (red2 if dst is red else red)
                assert src is red
                s.did(v.tensor_scalar(wrap[:], red[:], PI / 2, None, ALU.add))
                s.settle()
                s.did(v.tensor_scalar(red2[:], wrap[:], PI, -2 * PI, ALU.is_gt, ALU.mult))
                s.settle()
                s.did(v.tensor_tensor(wrap[:], wrap[:], red2[:], ALU.add))
                s.settle()
                s.did(v.tensor_scalar(wrap[:], wrap[:], PI_SAFE, -PI_SAFE, ALU.min, ALU.max))
                s.settle()
                v.tensor_scalar(red[:], red[:], PI_SAFE, -PI_SAFE, ALU.min, ALU.max).then_inc(q["rec_angle"], 1)
                dve.wait_ge(q["rec_rate"], 1)
                s.did(v.tensor_scalar(decay[:, :, 1:SEQ], decay[:, :, 1:SEQ], rate[:, 0:1], None, ALU.add))
                s.settle()

        VEC = 2 * Norm.STEPS + 10
        with nc.Block() as block:
            @block.tensor
            def _(pe):
                with pe.Fori(0, NBLK) as b:
                    pe.wait_ge(q["h2_ready"], b + 1)
                    hold(pe, core.passed)
                    for t in range(TILES):
                        last = nc.tensor.transpose(ps_T[:, t * P:(t + 1) * P], h2[:, t, :], ident[:])
                    last.then_inc(q["h2T_ps"], 1)
                    pe.wait_ge(q["h2T_ready"], b + 1)
                    for part in range(2):
                        for c in range(2):
                            cc = slice(c * HALF, (c + 1) * HALF)
                            last = nc.tensor.matmul(ps_u[:, part, cc], wiT[:, part, :], h2T[:, cc],
                                                    start=True, stop=True)
                    last.then_inc(q["u_ps"], 1)
                    pe.wait_ge(q["x_ready"], 2 * (b + 1))
                    for t in range(TILES):
                        for part, xx in enumerate((xr, xi)):
                            lhs = xx[:].rearrange("p i s -> p (i s)")[:, t * P:(t + 1) * P]
                            last = nc.tensor.matmul(ps_y[:, t, :], lhs, wog[:, part, :],
                                                    start=part == 0, stop=part == 1)
                    last.then_inc(q["y3_ps"], 1)
                    pe.wait_ge(q["h3_ready"], b + 1)
                    hold(pe, core.passed)
                    for t in range(TILES):
                        last = nc.tensor.transpose(ps_T[:, t * P:(t + 1) * P], h3[:, t, :], ident[:])
                    last.then_inc(q["h3T_ps"], 1)

            @block.scalar
            def _(act):
                with act.Fori(0, NBLK) as b:
                    act.wait_ge(q["squares2"], b + 1)
                    norm2.root(nc, eps[:, 0:1]).then_inc(q["root2"], 1)
                    act.wait_ge(q["h2T_ps"], b + 1)
                    nc.scalar.copy(h2T[:], ps_T[:]).then_inc(q["h2T_ready"], 1)
                    act.wait_ge(q["u_ps"], b + 1)
                    for part, uu in enumerate((ur, ui)):
                        nc.scalar.activation(uu[:].rearrange("p i s -> p (i s)"), ps_u[:, part, :],
                                             ACT.Identity, bias=bi[:, part:part + 1]).then_inc(q["u_ready"], 1)
                    act.wait_ge(q["squares3"], b + 1)
                    norm3.root(nc, eps[:, 0:1]).then_inc(q["root3"], 1)
                    act.wait_ge(q["h3T_ps"], b + 1)
                    nc.scalar.copy(hT[:, bass.ds(b * BLK, BLK)], ps_T[:]).then_inc(q["h3_stored"], 1)

            @block.gpsimd
            def _(pool):
                ci, si = spread(cos[:], 1, IMG), spread(sin[:], 1, IMG)
                with pool.Fori(0, NBLK) as b:
                    pool.tensor_copy(z2[:], H[:, bass.ds(b * TILES, TILES), :]).then_inc(q["z2_in"], 1)
                    pool.wait_ge(q["u_ready"], 2 * (b + 1))
                    pool.tensor_tensor(t2[:], ur[:], si, ALU.mult).then_inc(q["v_pool"], 1)
                    pool.wait_ge(q["scan_ready"], 2 * (b + 1))
                    pool.tensor_tensor(t2[:], yr[:], si, ALU.mult).then_inc(q["x_pool"], 1)
                    pool.wait_ge(q["h3_ready"], b + 1)
                    hold(pool, core.passed)
                    pool.tensor_copy(H[:, bass.ds(b * TILES, TILES), :], h3[:]).then_inc(q["h3_stored"], 1)

            @block.vector
            def _(dve):
                v = nc.vector
                ci, si = spread(cos[:], 1, IMG), spread(sin[:], 1, IMG)
                flat = "p i s -> p (i s)"
                with dve.Fori(0, NBLK) as b:
                    s = Steps(dve, q["rec_step"], b * VEC)
                    dve.wait_ge(q["z2_in"], b + 1)
                    norm2.center(nc, s, z2[:]).then_inc(q["squares2"], 1)
                    dve.wait_ge(q["root2"], b + 1)
                    norm2.divide(nc, s, h2[:]).then_inc(q["h2_ready"], 1)
                    dve.wait_ge(q["h2_ready"], b + 1)
                    s.did(v.tensor_tensor(h2b[:], h2[:], spread(row["bo"], 1, TILES), ALU.add))
                    dve.wait_ge(q["u_ready"], 2 * (b + 1))
                    s.did(v.tensor_tensor(t1[:], ui[:], si, ALU.mult))
                    s.did(v.tensor_tensor(vr[:], ur[:], ci, ALU.mult))
                    s.did(v.tensor_tensor(vi[:], ui[:], ci, ALU.mult))
                    s.settle()
                    s.did(v.tensor_tensor(vr[:], vr[:], t1[:], ALU.add))
                    dve.wait_ge(q["v_pool"], b + 1)
                    s.did(v.tensor_tensor(vi[:], vi[:], t2[:], ALU.subtract))
                    s.settle()
                    for yy, vv in ((yr, vr), (yi, vi)):
                        v.tensor_tensor_scan(yy[:].rearrange(flat), decay[:].rearrange(flat),
                                             vv[:].rearrange(flat), 0.0, ALU.mult, ALU.add
                                             ).then_inc(q["scan_ready"], 1)
                    dve.wait_ge(q["scan_ready"], 2 * (b + 1))
                    s.did(v.tensor_tensor(t1[:], yi[:], si, ALU.mult))
                    s.did(v.tensor_tensor(xr[:], yr[:], ci, ALU.mult))
                    s.did(v.tensor_tensor(xi[:], yi[:], ci, ALU.mult))
                    s.settle()
                    v.tensor_tensor(xr[:], xr[:], t1[:], ALU.subtract).then_inc(q["x_ready"], 1)
                    dve.wait_ge(q["x_pool"], b + 1)
                    v.tensor_tensor(xi[:], xi[:], t2[:], ALU.add).then_inc(q["x_ready"], 1)
                    dve.wait_ge(q["y3_ps"], b + 1)
                    s.did(v.tensor_tensor(z3[:], ps_y[:], h2b[:], ALU.add))
                    s.settle()
                    norm3.center(nc, s, z3[:]).then_inc(q["squares3"], 1)
                    dve.wait_ge(q["root3"], b + 1)
                    norm3.divide(nc, s, h3[:]).then_inc(q["h3_ready"], 1)
                    dve.wait_ge(q["h3_stored"], 2 * (b + 1))
                    assert s.n == VEC, s.n


def experts(core, out):
    nc, ins = core.nc, core.inputs
    hT, H, ident, eps, row = core.hT, core.H, core.ident, core.eps, core.row
    with ExitStack() as scope:
        def sb(name, shape, dt=F32):
            return core.sb(name, shape, dt, scope)

        gate_w = sb("gate_w", [D, EXP])
        w1 = sb("w1", [D, EXP, FF])
        b1 = sb("b1e", [FF, EXP])
        w2 = sb("w2", [FF, EXP, D])
        b2 = sb("b2e", [EXP, D])
        xT = sb("xT", [D, BLK])
        x3 = sb("x3", [P, TILES, D])
        lg = sb("lg", [P, TILES, EXP])
        best = sb("best", [P, TILES, 8])
        rel = sb("rel", [P, TILES, EXP])
        rel_exp = sb("rel_exp", [P, TILES, EXP])
        chosen = sb("chosen", [P, TILES, EXP])
        gate = sb("gate", [P, TILES, EXP])
        gsum = sb("gsum", [P, TILES])
        grec = sb("grec", [P, TILES])
        gateT = sb("gateT", [EXP, BLK])
        hidden = [sb(f"hidden{i}", [FF, EXP, HALF]) for i in range(2)]
        gated = [sb(f"gated{i}", [P, EXP, D]) for i in range(2)]
        moe = sb("moe", [P, TILES, D])
        z4 = sb("z4", [P, TILES, D])
        n4 = sb("n4", [P, TILES, D])
        z5 = sb("z5", [P, TILES, D])
        res = sb("res", [P, TILES, D])
        norm4 = Norm(sb, "norm4")
        norm5 = Norm(sb, "norm5")
        ps_g = core.ps("ps_g", [P, 512], scope)
        ps_h = [core.ps(f"ps_h{i}", [FF, HALF], scope) for i in range(3)]
        ps_e = [core.ps(f"ps_e{i}", [P, EXP, D], scope) for i in range(2)]

        names = """exp_w_in exp_step block_in gates_ps gates_in gates_exp gates_ready gateT_ps
            gateT_ready b2_ps hid_ps hid_ready exp_ps exp_free moe_ready squares4 root4 squares5
            root5 result_ready stored"""
        q = {n: core.sem(n) for n in names.split()}
        HPB = 2 * EXP
        VEC = 2 * TILES + 2 * Norm.STEPS + 12

        with nc.Block() as block:
            @block.sync
            def _(sp):
                for dst, name in ((gate_w, "gate_w"), (w1, "ew1"), (b1, "eb1"), (w2, "ew2"), (b2, "eb2")):
                    sp.dma_start(dst[:], ins[name]).then_inc(q["exp_w_in"], 16)
                with sp.Fori(0, NBLK) as b:
                    sp.wait_ge(q["result_ready"], b + 1)
                    sp.dma_start(out[:, bass.ds(b * TILES, TILES), :], res[:]).then_inc(q["stored"], 16)
                sp.wait_ge(q["stored"], 16 * NBLK)

            @block.gpsimd
            def _(pool):
                with pool.Fori(0, NBLK) as b:
                    pool.wait_ge(q["exp_free"], b + 1)
                    hold(pool, core.passed)
                    pool.tensor_copy(xT[:], hT[:, bass.ds(b * BLK, BLK)]).then_inc(q["block_in"], 1)
                    pool.tensor_copy(x3[:], H[:, bass.ds(b * TILES, TILES), :]).then_inc(q["block_in"], 1)

            @block.tensor
            def _(pe):
                mm = nc.tensor.matmul
                pe.wait_ge(q["exp_w_in"], 80)
                with pe.Fori(0, NBLK) as b:
                    pe.wait_ge(q["block_in"], 2 * (b + 1))
                    for t in range(TILES):
                        last = mm(ps_g[:, t * EXP:(t + 1) * EXP], xT[:, t * P:(t + 1) * P], gate_w[:],
                                  start=True, stop=True)
                    last.then_inc(q["gates_ps"], 1)
                    for half in range(2):
                        for e in range(EXP):
                            n = half * EXP + e
                            if n >= 3:
                                pe.wait_ge(q["hid_ready"], b * HPB + (n - 2))
                            mm(ps_h[n % 3][:], w1[:, e, :], xT[:, half * HALF:(half + 1) * HALF],
                               start=True, stop=True).then_inc(q["hid_ps"], 1)
                        if half == 0:
                            pe.wait_ge(q["gates_ready"], b + 1)
                            hold(pe, core.passed)
                            for t in range(4):
                                last = nc.tensor.transpose(ps_g[0:EXP, t * P:(t + 1) * P], gate[:, t, :],
                                                           ident[:])
                            last.then_inc(q["gateT_ps"], 1)
                            pe.wait_ge(q["gateT_ready"], 2 * b + 1)
                            hold(pe, core.passed)
                            for t in range(4, TILES):
                                last = nc.tensor.transpose(ps_g[0:EXP, (t - 4) * P:(t - 3) * P],
                                                           gate[:, t, :], ident[:])
                            last.then_inc(q["gateT_ps"], 1)
                            pe.wait_ge(q["gateT_ready"], 2 * b + 2)
                            for t in range(TILES):
                                last = mm(ps_g[:, t * D:(t + 1) * D], gateT[:, t * P:(t + 1) * P], b2[:],
                                          start=True, stop=True)
                            last.then_inc(q["b2_ps"], 1)
                        pe.wait_ge(q["hid_ready"], b * HPB + (half + 1) * EXP)
                        for t in range(4):
                            n = half * 4 + t
                            if n >= 2:
                                pe.wait_ge(q["moe_ready"], b * TILES + (n - 1))
                            for e in range(EXP):
                                last = mm(ps_e[n % 2][:, e, :], hidden[half][:, e, t * P:(t + 1) * P],
                                          w2[:, e, :], start=True, stop=True)
                            last.then_inc(q["exp_ps"], 1)

            @block.scalar
            def _(act):
                with act.Fori(0, NBLK) as b:
                    for half in range(2):
                        for e in range(EXP):
                            n = half * EXP + e
                            act.wait_ge(q["hid_ps"], b * HPB + (n + 1))
                            nc.scalar.activation(hidden[half][:, e, :], ps_h[n % 3][:], ACT.Relu,
                                                 bias=b1[:, e:e + 1]).then_inc(q["hid_ready"], 1)
                            if half == 0 and e == 4:
                                act.wait_ge(q["gates_in"], b + 1)
                                nc.scalar.activation(rel_exp[:], rel[:], ACT.Exp).then_inc(q["gates_exp"], 1)
                        if half == 0:
                            for part in range(2):
                                act.wait_ge(q["gateT_ps"], 2 * b + (part + 1))
                                nc.scalar.copy(gateT[:, part * HALF:(part + 1) * HALF],
                                               ps_g[0:EXP, :]).then_inc(q["gateT_ready"], 1)
                    act.wait_ge(q["squares4"], b + 1)
                    norm4.root(nc, eps[:, 0:1]).then_inc(q["root4"], 1)
                    act.wait_ge(q["squares5"], b + 1)
                    norm5.root(nc, eps[:, 0:1]).then_inc(q["root5"], 1)

            @block.vector
            def _(dve):
                v = nc.vector
                dve.sem_inc(q["exp_free"], 1)
                with dve.Fori(0, NBLK) as b:
                    s = Steps(dve, q["exp_step"], b * VEC)
                    dve.wait_ge(q["gates_ps"], b + 1)
                    s.did(v.tensor_tensor(lg[:], ps_g[:, 0:TILES * EXP].rearrange("p (t e) -> p t e", e=EXP),
                                          spread(row["gate_b"], 1, TILES), ALU.add))
                    s.settle()
                    hold(dve, core.passed)
                    for t in range(TILES):
                        s.did(v.max(best[:, t, :], lg[:, t, :]))
                    s.settle()
                    v.tensor_tensor(rel[:], lg[:], spread(best[:, :, 0], 2, EXP), ALU.subtract
                                    ).then_inc(q["gates_in"], 1)
                    s.did(v.tensor_tensor(chosen[:], lg[:], spread(best[:, :, 1], 2, EXP), ALU.is_ge))
                    s.settle()
                    dve.wait_ge(q["gates_exp"], b + 1)
                    s.did(v.tensor_tensor(chosen[:], chosen[:], rel_exp[:], ALU.mult))
                    s.settle()
                    s.did(v.reduce_sum(gsum[:], chosen[:], axis=AX))
                    s.settle()
                    s.did(v.reciprocal(grec[:], gsum[:]))
                    s.settle()
                    v.tensor_tensor(gate[:], chosen[:], spread(grec[:], 2, EXP), ALU.mult
                                    ).then_inc(q["gates_ready"], 1)
                    dve.wait_ge(q["b2_ps"], b + 1)
                    s.did(v.tensor_tensor(z4[:], x3[:], ps_g[:].rearrange("p (t d) -> p t d", d=D), ALU.add))
                    for t in range(TILES):
                        dve.wait_ge(q["exp_ps"], b * TILES + (t + 1))
                        v.tensor_tensor(gated[t % 2][:], ps_e[t % 2][:], spread(gate[:, t, :], 2, D),
                                        ALU.mult).then_inc(q["moe_ready"], 1)
                        dve.wait_ge(q["moe_ready"], b * TILES + (t + 1))
                        s.did(v.reduce_sum(moe[:, t, :], gated[t % 2][:].rearrange("p e d -> p d e"), axis=AX))
                    s.settle()
                    s.did(v.tensor_tensor(z4[:], z4[:], moe[:], ALU.add))
                    s.settle()
                    norm4.center(nc, s, z4[:]).then_inc(q["squares4"], 1)
                    dve.wait_ge(q["root4"], b + 1)
                    s.did(norm4.divide(nc, s, n4[:]))
                    s.settle()
                    s.did(v.tensor_tensor(n4[:], n4[:], spread(row["ln_gamma"], 1, TILES), ALU.mult))
                    s.settle()
                    s.did(v.tensor_tensor(n4[:], n4[:], spread(row["ln_beta"], 1, TILES), ALU.add))
                    s.settle()
                    s.did(v.tensor_tensor(z5[:], n4[:], x3[:], ALU.add))
                    s.settle()
                    dve.sem_inc(q["exp_free"], 1)
                    norm5.center(nc, s, z5[:]).then_inc(q["squares5"], 1)
                    dve.wait_ge(q["root5"], b + 1)
                    s.did(norm5.divide(nc, s, res[:]))
                    s.settle()
                    dve.sem_inc(q["result_ready"], 1)
                    dve.wait_ge(q["stored"], 16 * (b + 1))
                    assert s.n == VEC, (s.n, VEC)


def kernel(**inputs):
    import numpy as np
    import concourse.bacc as bacc
    from concourse.bass_utils import run_bass_kernel_spmd

    a = {k: np.asarray(v) for k, v in inputs.items()}
    c = np.ascontiguousarray
    tab = np.concatenate([a["L0_ffn_keys_table"], a["L0_ffn_values_table"]], axis=1)
    tab = tab.reshape(HEADS, 2, PER_Q, 4, 2, 32, 2 * D).transpose(3, 5, 0, 4, 1, 2, 6)
    wqpk = a["L0_ffn_Wq_pk"].reshape(D, 2 * HEADS, KD)
    pk = a["L0_ffn_pk_keys"]
    arrays = {
        "x": a["x"].reshape(TOK // P, P, D * 4).transpose(1, 0, 2),
        "tokw": np.concatenate([a["L0_tok_W"], a["L0_tok_b"][:, None]], axis=1),
        "cols": np.stack([a["L0_attn_" + n] for n in COLS], axis=1),
        "bmcm": np.stack([a["L0_attn_Bm"], a["L0_attn_Cm"]], axis=1),
        "taps": a["L0_attn_wd"].reshape(E, TAPS),
        "w1T": a["L0_attn_w1"].T,
        "w2T": a["L0_attn_w2"].T,
        "rows": np.concatenate([a["L0_attn_b2"], a["L1_attn_bo"], a["L1_ffn_gate_b"],
                                a["L1_ffn_gamma"], a["L1_ffn_beta"]])[None, :],
        "wqpkT": wqpk.transpose(2, 1, 0),
        "keysT": pk.transpose(3, 0, 2, 1).reshape(KD, 2 * HEADS, NK),
        "wq": a["L0_ffn_Wq"],
        "wo": a["L0_ffn_Wo"].reshape(HEADS, D, D).transpose(1, 0, 2),
        "table": tab.reshape(P, HEADS * QUARTERS, PER_Q * 2 * D),
        "wiT": a["L1_attn_Wi"].reshape(2, N, D).transpose(2, 0, 1),
        "bi": a["L1_attn_bi"].reshape(2, N).T,
        "woT": a["L1_attn_Wo"].reshape(D, 2, N).transpose(2, 1, 0),
        "plog": a["L1_attn_params_log"].T,
        "gate_w": a["L1_ffn_gate_w"],
        "ew1": a["L1_ffn_w1"].transpose(1, 0, 2),
        "eb1": a["L1_ffn_b1"].T,
        "ew2": a["L1_ffn_w2"].transpose(1, 0, 2),
        "eb2": a["L1_ffn_b2"],
    }
    nc = bacc.Bacc("TRN2", target_bir_lowering=False, num_devices=1)
    feed, aps = {}, {}
    for name, value in arrays.items():
        feed["in_" + name] = c(value)
        aps[name] = nc.dram_tensor("in_" + name, value.shape, mybir.dt.from_np(value.dtype),
                                   kind="ExternalInput").ap()
    out = nc.dram_tensor("out_tokens", (P, TOK // P, D), F32, kind="ExternalOutput").ap()
    program(nc, aps, out)
    r = run_bass_kernel_spmd(nc, [feed], core_ids=[0])
    got = r.results[0]["out_tokens"]
    return np.ascontiguousarray(got.transpose(1, 0, 2)).reshape(IMAGES, SEQ, D)
```

```python
from contextlib import ExitStack

import concourse.bass as bass
from concourse import mybir

F32 = mybir.dt.float32
F32R = mybir.dt.float32r
ALU = mybir.AluOpType
ACT = mybir.ActivationFunctionType
AX = mybir.AxisListType.X

P = 128
IMAGES, SEQ, D = 128, 64, 64
TOK = IMAGES * SEQ
BLK = 1024
HALF = BLK // 2
NBLK = TOK // BLK
TILES = BLK // P
IMG = BLK // SEQ
E = 128
TAPS = 5
HEADS = 8
NK = 64
KD = 32
TOPK = 16
UNITS = NBLK * HEADS
PAIRS = UNITS // 2
CHUNKS = 32
PER_Q = 8
QUARTERS = CHUNKS // PER_Q
STEPS = 2 * CHUNKS
LAG = 3
BIG = 1e30
LOG_TINY = 87.3
SHIFT = LOG_TINY / 2
EPS = 1e-5
N = 128
EXP = 16
FF = 128
PI = 3.141592653589793
PI_SAFE = 3.1415925
CAND_BLOCKS = ((0, 1, 17), (1, 3, 8), (4, 13, 3))
NCAND = sum(na * nb for _, na, nb in CAND_BLOCKS)
LISTED = 24
ROWS = (("b2", D), ("bo", D), ("gate_b", EXP), ("ln_gamma", D), ("ln_beta", D))
NROW = sum(n for _, n in ROWS)
COLS = ("b1", "bd", "gamma", "beta", "rmean", "rvar", "A", "Dv")


def spread(ap, axis, n):
    u = ap.unsqueeze(axis)
    shape = list(u.shape)
    shape[axis] = n
    return u.broadcast_to(shape)


def hold(engine, passed):
    engine.sem_inc(passed, 1)


def store_low(nc, hT, b, x):
    return nc.vector.tensor_tensor(hT[D:P, bass.ds(b * BLK, BLK)], x[:],
                                   hT[0:D, bass.ds(b * BLK, BLK)].bitcast(F32), ALU.subtract)


def split(nc, s, parts, x):
    s.did(nc.vector.tensor_copy(parts[:, 0], x))
    s.settle()
    s.did(nc.vector.tensor_tensor(parts[:, 1], x, parts[:, 0].bitcast(F32), ALU.subtract))


class Steps:

    def __init__(self, engine, sem, base=0):
        self.engine, self.sem, self.base, self.n = engine, sem, base, 0

    def did(self, instruction):
        instruction.then_inc(self.sem, 1)
        self.n += 1

    def settle(self):
        self.engine.wait_ge(self.sem, self.base + self.n)


class Norm:
    STEPS = 4

    def __init__(self, sb, name):
        self.mean = sb(name + "_mean", [P, TILES])
        self.centered = sb(name + "_centered", [P, TILES, D])
        self.square = sb(name + "_square", [P, TILES, D])
        self.sumsq = sb(name + "_sumsq", [P, TILES])
        self.std = sb(name + "_std", [P, TILES])
        self.rstd = sb(name + "_rstd", [P, TILES])

    def center(self, nc, s, z):
        v = nc.vector
        s.did(v.reduce_sum(self.mean[:], z, axis=AX))
        s.settle()
        s.did(v.scalar_tensor_tensor(self.centered[:], spread(self.mean[:], 2, D), -1.0 / D, z,
                                     ALU.mult, ALU.add))
        s.settle()
        s.did(v.tensor_tensor(self.square[:], self.centered[:], self.centered[:], ALU.mult))
        s.settle()
        return v.reduce_sum(self.sumsq[:], self.square[:], axis=AX)

    def root(self, nc, eps):
        return nc.scalar.activation(self.std[:], self.sumsq[:], ACT.Sqrt, bias=eps, scale=1.0 / D)

    def divide(self, nc, s, out):
        s.did(nc.vector.reciprocal(self.rstd[:], self.std[:]))
        s.settle()
        return nc.vector.tensor_tensor(out, self.centered[:], spread(self.rstd[:], 2, D), ALU.mult)


class Core:

    def __init__(self, nc, stack, inputs):
        self.nc, self.stack, self.inputs = nc, stack, inputs
        self.hT = self.sb("hT", [P, TOK], F32R)
        self.H = self.sb("H", [P, TOK // P, D])
        self.ident = self.sb("ident", [P, P])
        self.eps = self.sb("eps", [P, 1])
        self.passed = self.sem("passed")
        self.rowb = self.sb("rowb", [P, NROW])
        self.row, at = {}, 0
        for name, n in ROWS:
            self.row[name] = self.rowb[:, at:at + n]
            at += n

    def sb(self, name, shape, dt=F32, stack=None):
        return (stack or self.stack).enter_context(self.nc.sbuf_tensor(name, shape, dt))

    def ps(self, name, shape, stack):
        return stack.enter_context(self.nc.psum_tensor(name, shape, F32))

    def sem(self, name):
        return self.stack.enter_context(self.nc.semaphore(name))


def program(nc, inputs, out):
    with ExitStack() as stack:
        core = Core(nc, stack, inputs)
        mixer(core)
        memory(core)
        recurrent(core)
        experts(core, out)
    return nc


def mixer(core):
    nc, ins = core.nc, core.inputs
    hT, H, ident, eps, rowb, row = core.hT, core.H, core.ident, core.eps, core.rowb, core.row
    with ExitStack() as scope:
        def sb(name, shape, dt=F32):
            return core.sb(name, shape, dt, scope)

        tokw = sb("tokw", [E, 5])
        cols = sb("cols", [E, len(COLS)])
        col = {n: cols[:, i:i + 1] for i, n in enumerate(COLS)}
        bmcm = sb("bmcm", [E, 2, 8])
        taps = sb("taps", [E, TAPS])
        w1T = sb("w1T", [D, E])
        w2T = sb("w2T", [E, D])
        rows = sb("rows", [1, NROW])
        mean_w = sb("mean_w", [E, P])
        ones_row = sb("ones_row", [1, P])
        tokb = sb("tokb", [P, 5])
        w2state = sb("w2state", [E, D])
        w2skip = sb("w2skip", [E, D])
        bc = sb("bc", [E, 1])
        bcprod = sb("bcprod", [E, 8])
        bnstd = sb("bnstd", [E, 1])
        bninv = sb("bninv", [E, 1])
        bnscale = sb("bnscale", [E, 1])
        bnbias = sb("bnbias", [E, 1])
        bntmp = sb("bntmp", [E, 1])
        exp_a = sb("exp_a", [E, 1])
        decay = sb("decay", [E, IMG, SEQ])
        X = sb("X", [P, TILES, D, 4])
        h0 = sb("h0", [P, TILES, D])
        h0b = sb("h0b", [P, TILES, D])
        h0T = sb("h0T", [D, BLK])
        padded = sb("padded", [E, IMG, SEQ + TAPS - 1])
        conv = sb("conv", [E, IMG, SEQ])
        local = sb("local", [E, BLK])
        state = sb("state", [E, BLK])
        z = sb("z", [P, TILES, D])
        h1 = sb("h1", [P, TILES, D])
        norm = Norm(sb, "norm1")
        ps_small = core.ps("ps_small", [P, 512], scope)
        ps_T = core.ps("ps_T", [D, BLK], scope)
        ps_wide = core.ps("ps_wide", [E, BLK], scope)
        ps_out = core.ps("ps_out", [P, TILES, D], scope)

        weights_in = core.sem("weights_in")
        cleared = core.sem("cleared")
        consts = core.sem("consts")
        prep_step = core.sem("prep_step")
        means_ps = core.sem("means_ps")
        bn_root = core.sem("bn_root")
        decay_exp = core.sem("decay_exp")
        mix_step = core.sem("mix_step")
        x_in = core.sem("x_in")
        h0_ready = core.sem("h0_ready")
        h0T_ps = core.sem("h0T_ps")
        h0T_ready = core.sem("h0T_ready")
        wide_ps = core.sem("wide_ps")
        gated = core.sem("gated")
        conv_ready = core.sem("conv_ready")
        local_ready = core.sem("local_ready")
        state_ready = core.sem("state_ready")
        out_ps = core.sem("out_ps")
        squares1 = core.sem("squares1")
        root1 = core.sem("root1")
        h1_ready = core.sem("h1_ready")
        h1T_ps = core.sem("h1T_ps")
        h1_high = core.sem("h1_high")
        h1_stored = core.sem("h1_stored")

        LOADS = 7
        CLEARS = 5
        with nc.Block() as block:
            @block.sync
            def _(sp):
                for dst, name in ((tokw, "tokw"), (cols, "cols"), (bmcm, "bmcm"), (taps, "taps"),
                                  (w1T, "w1T"), (w2T, "w2T"), (rows, "rows")):
                    sp.dma_start(dst[:], ins[name]).then_inc(weights_in, 16)

            @block.gpsimd
            def _(pool):
                for t, value in ((ident, 0.0), (decay, 0.0), (padded, 0.0), (mean_w, 1.0 / E),
                                 (ones_row, 1.0)):
                    pool.memset(t[:], value).then_inc(cleared, 1)
                pool.memset(eps[:], EPS).then_inc(consts, 1)
                pool.wait_ge(cleared, CLEARS)
                pool.affine_select(out=ident[:], in_=ident[:], compare_op=ALU.not_equal, fill=1.0,
                                   base=0, pattern=[[-1, P]], channel_multiplier=1).then_inc(consts, 1)

            @block.tensor
            def _(pe):
                pe.wait_ge(weights_in, 16 * LOADS)
                pe.wait_ge(cleared, CLEARS)
                nc.tensor.matmul(ps_small[:, 0:5], mean_w[:], tokw[:], start=True, stop=True)
                nc.tensor.matmul(ps_small[:, 8:8 + NROW], ones_row[:], rows[:],
                                 start=True, stop=True).then_inc(means_ps, 1)

            @block.scalar
            def _(act):
                act.wait_ge(weights_in, 16 * LOADS)
                nc.scalar.activation(exp_a[:], col["A"], ACT.Exp).then_inc(decay_exp, 1)
                act.wait_ge(consts, 2)
                nc.scalar.activation(bnstd[:], col["rvar"], ACT.Sqrt, bias=eps[:, 0:1]).then_inc(bn_root, 1)

            @block.vector
            def _(dve):
                v = nc.vector
                s = Steps(dve, prep_step)
                dve.wait_ge(weights_in, 16 * LOADS)
                s.did(v.tensor_tensor(bcprod[:], bmcm[:, 0], bmcm[:, 1], ALU.mult))
                s.did(v.tensor_scalar(w2skip[:], w2T[:], col["Dv"], None, ALU.mult))
                s.settle()
                s.did(v.reduce_sum(bc[:], bcprod[:], axis=AX))
                s.settle()
                s.did(v.tensor_scalar(w2state[:], w2T[:], bc[:, 0:1], None, ALU.mult))
                dve.wait_ge(bn_root, 1)
                s.did(v.reciprocal(bninv[:], bnstd[:]))
                s.did(v.tensor_tensor(bntmp[:], col["bd"], col["rmean"], ALU.subtract))
                s.settle()
                s.did(v.tensor_tensor(bnscale[:], bninv[:], col["gamma"], ALU.mult))
                s.settle()
                s.did(v.scalar_tensor_tensor(bnbias[:], bntmp[:], bnscale[:, 0:1], col["beta"],
                                             ALU.mult, ALU.add))
                dve.wait_ge(decay_exp, 1)
                dve.wait_ge(cleared, CLEARS)
                s.did(v.tensor_scalar(decay[:, :, 1:SEQ], decay[:, :, 1:SEQ], exp_a[:, 0:1], None, ALU.add))
                dve.wait_ge(means_ps, 1)
                s.did(v.tensor_copy(tokb[:], ps_small[:, 0:5]))
                s.did(v.tensor_copy(rowb[:], ps_small[:, 8:8 + NROW]))
                s.settle()

        FRONT, BACK = 3, (TAPS - 1) + 1 + Norm.STEPS + 1
        LOOPED = NBLK - 1
        with nc.Block() as block:
            @block.sync
            def _(sp):
                def load(b):
                    sp.dma_start(X[:].rearrange("p t j f -> p t (j f)"),
                                 ins["x"][:, bass.ds(b * TILES, TILES), :]).then_inc(x_in, 16)

                load(0)
                with sp.Fori(1, NBLK) as b:
                    sp.wait_ge(h0_ready, b)
                    load(b)

            @block.tensor
            def _(pe):
                def features_first(b):
                    pe.wait_ge(h0_ready, b + 1)
                    hold(pe, core.passed)
                    for t in range(TILES):
                        last = nc.tensor.transpose(ps_T[:, t * P:(t + 1) * P], h0[:, t, :], ident[:])
                    last.then_inc(h0T_ps, 1)

                def expand(b):
                    pe.wait_ge(h0T_ready, b + 1)
                    for c in range(2):
                        cc = slice(c * HALF, (c + 1) * HALF)
                        last = nc.tensor.matmul(ps_wide[:, cc], w1T[:], h0T[:, cc], start=True, stop=True)
                    last.then_inc(wide_ps, 1)

                def project(b):
                    pe.wait_ge(state_ready, b + 1)
                    for t in range(TILES):
                        tt = slice(t * P, (t + 1) * P)
                        nc.tensor.matmul(ps_out[:, t, :], state[:, tt], w2state[:], start=True, stop=False)
                        last = nc.tensor.matmul(ps_out[:, t, :], local[:, tt], w2skip[:],
                                                start=False, stop=True)
                    last.then_inc(out_ps, 1)

                def result_features(b):
                    pe.wait_ge(h1_ready, b + 1)
                    hold(pe, core.passed)
                    for t in range(TILES):
                        last = nc.tensor.transpose(ps_T[:, t * P:(t + 1) * P], h1[:, t, :], ident[:])
                    last.then_inc(h1T_ps, 1)

                features_first(0)
                expand(0)
                with pe.Fori(0, LOOPED) as b:
                    features_first(b + 1)
                    project(b)
                    expand(b + 1)
                    result_features(b)
                project(NBLK - 1)
                result_features(NBLK - 1)

            @block.scalar
            def _(act):
                def gate(b):
                    act.wait_ge(h0T_ps, b + 1)
                    nc.scalar.copy(h0T[:], ps_T[:]).then_inc(h0T_ready, 1)
                    act.wait_ge(wide_ps, b + 1)
                    nc.scalar.activation(padded[:, :, 2:2 + SEQ],
                                         ps_wide[:].rearrange("p (i s) -> p i s", s=SEQ),
                                         ACT.Silu, bias=col["b1"]).then_inc(gated, 1)

                def normalize(b):
                    act.wait_ge(conv_ready, b + 1)
                    nc.scalar.activation(local[:], conv[:].rearrange("p i s -> p (i s)"), ACT.Silu,
                                         bias=bnbias[:, 0:1], scale=bnscale[:, 0:1]).then_inc(local_ready, 1)

                def store(b):
                    act.wait_ge(squares1, b + 1)
                    norm.root(nc, eps[:, 0:1]).then_inc(root1, 1)
                    act.wait_ge(h1T_ps, b + 1)
                    nc.scalar.copy(hT[0:D, bass.ds(b * BLK, BLK)], ps_T[:]).then_inc(h1_high, 1)

                gate(0)
                with act.Fori(0, LOOPED) as b:
                    normalize(b)
                    gate(b + 1)
                    store(b)
                normalize(NBLK - 1)
                store(NBLK - 1)

            @block.gpsimd
            def _(pool):
                with pool.Fori(0, NBLK) as b:
                    pool.wait_ge(h1_ready, b + 1)
                    hold(pool, core.passed)
                    pool.tensor_copy(H[:, bass.ds(b * TILES, TILES), :], h1[:]).then_inc(h1_stored, 1)

            @block.vector
            def _(dve):
                v = nc.vector

                def token_bias(s, b):
                    dve.wait_ge(x_in, 16 * (b + 1))
                    s.did(v.tensor_scalar(h0[:], X[:, :, :, 0], tokb[:, 0:1], tokb[:, 4:5], ALU.mult, ALU.add))
                    for f in (1, 2):
                        s.settle()
                        s.did(v.scalar_tensor_tensor(h0[:], X[:, :, :, f], tokb[:, f:f + 1], h0[:],
                                                     ALU.mult, ALU.add))
                    s.settle()
                    v.scalar_tensor_tensor(h0[:], X[:, :, :, 3], tokb[:, 3:4], h0[:],
                                           ALU.mult, ALU.add).then_inc(h0_ready, 1)

                def residual(s, b):
                    dve.wait_ge(h0_ready, b + 1)
                    s.did(v.tensor_tensor(h0b[:], h0[:], spread(row["b2"], 1, TILES), ALU.add))

                def low(b):
                    dve.wait_ge(h1_high, b + 1)
                    store_low(nc, hT, b, ps_T).then_inc(h1_stored, 1)

                def iteration(s, b, first=False, last=False):
                    dve.wait_ge(gated, b + 1)
                    s.did(v.tensor_scalar(conv[:], padded[:, :, 0:SEQ], taps[:, 0:1], None, ALU.mult))
                    for k in range(1, TAPS - 1):
                        s.settle()
                        s.did(v.scalar_tensor_tensor(conv[:], padded[:, :, k:k + SEQ], taps[:, k:k + 1],
                                                     conv[:], ALU.mult, ALU.add))
                    s.settle()
                    v.scalar_tensor_tensor(conv[:], padded[:, :, TAPS - 1:TAPS - 1 + SEQ],
                                           taps[:, TAPS - 1:TAPS], conv[:],
                                           ALU.mult, ALU.add).then_inc(conv_ready, 1)
                    if not first:
                        low(b - 1)
                    if not last:
                        token_bias(s, b + 1)
                    dve.wait_ge(local_ready, b + 1)
                    v.tensor_tensor_scan(state[:], decay[:].rearrange("p i s -> p (i s)"), local[:], 0.0,
                                         ALU.mult, ALU.add).then_inc(state_ready, 1)
                    dve.wait_ge(out_ps, b + 1)
                    s.did(v.tensor_tensor(z[:], ps_out[:], h0b[:], ALU.add))
                    s.settle()
                    norm.center(nc, s, z[:]).then_inc(squares1, 1)
                    if not last:
                        residual(s, b + 1)
                    dve.wait_ge(root1, b + 1)
                    if not first:
                        dve.wait_ge(h1_stored, 2 * b)
                    norm.divide(nc, s, h1[:]).then_inc(h1_ready, 1)

                s = Steps(dve, mix_step)
                token_bias(s, 0)
                residual(s, 0)
                iteration(s, 0, first=True)
                before = s.n
                assert before == 2 * FRONT + 1 + BACK, before
                with dve.Fori(1, LOOPED) as b:
                    s = Steps(dve, mix_step, before + (b - 1) * (FRONT + BACK))
                    iteration(s, b)
                    assert s.n == FRONT + BACK, s.n
                s = Steps(dve, mix_step, before + (LOOPED - 1) * (FRONT + BACK))
                iteration(s, NBLK - 1, last=True)
                low(NBLK - 1)



def memory(core):
    nc, ins = core.nc, core.inputs
    hT, H, ident = core.hT, core.H, core.ident
    with ExitStack() as scope:
        def sb(name, shape, dt=F32):
            return core.sb(name, shape, dt, scope)

        score_w = sb("score_w", [P, 2, HEADS, 2 * NK], F32R)
        wq_all = sb("wq_all", [P, 2, HEADS * D], F32R)
        lower = sb("lower", [P, P], F32R)
        causal = sb("causal", [P, SEQ])
        pick = sb("pick", [P, PER_Q, P], F32R)
        probs = sb("probs", [P, TILES, P])
        shift = sb("shift", [P, 1])

        psS = [core.ps(f"psS{i}", [P, HALF], scope) for i in range(LAG + 1)]
        acc = core.ps("acc", [P, BLK], scope)
        side = core.ps("side", [P, BLK], scope)

        names = """keys_in masks_cleared masks_made pick_made score_w_ps mem_prep
            staged wo_in sims_ps sims_ready mem_step exp_in exp_done thr_ready diag_ready q_ps q_ready
            scores_ps hi_ready lo_ready s_ready e_ready w_ready w_used acc_copied kv_ps kv_ready kT_ps
            kT_ready logits_ps logits_ready probs_ready probsT_ps probsT_ready y_ps y_ready y_added"""
        q = {n: core.sem(n) for n in names.split()}
        scores_in = [core.sem(f"scores_in{i}") for i in range(2)]
        table_in = [core.sem(f"table_in{i}") for i in range(QUARTERS)]

        with ExitStack() as early_scope:
            def early(name, shape, dt=F32):
                return core.sb(name, shape, dt, early_scope)

            wqp = early("wqp", [KD, 2 * HEADS, 2, D])
            keys = early("keys", [KD, 2 * HEADS, NK])
            wq_in = early("wq_in", [P, HEADS * D])
            causal2 = early("causal2", [P, 2, SEQ])
            lower32 = early("lower32", [P, P])
            pick32 = early("pick32", [P, PER_Q, 4, 32])

            with nc.Block() as block:
                @block.sync
                def _(sp):
                    for i in range(2):
                        sp.dma_start(wqp[:, :, i, :], ins["wqpkT"]).then_inc(q["keys_in"], 16)
                        sp.dma_start(wq_in[i * D:(i + 1) * D, :], ins["wq"]).then_inc(q["keys_in"], 16)
                    sp.dma_start(keys[:], ins["keysT"]).then_inc(q["keys_in"], 16)

                @block.gpsimd
                def _(pool):
                    pool.memset(lower32[:, 0:NK], 0.0).then_inc(q["masks_cleared"], 1)
                    pool.memset(lower32[:, NK:P], 1.0).then_inc(q["masks_cleared"], 1)
                    pool.memset(causal2[:], 0.0).then_inc(q["masks_cleared"], 1)
                    pool.memset(pick32[:], 0.0).then_inc(q["masks_cleared"], 1)
                    pool.memset(probs[:], 0.0).then_inc(q["masks_cleared"], 1)
                    pool.memset(shift[:], -SHIFT).then_inc(q["masks_cleared"], 1)
                    pool.wait_ge(q["masks_cleared"], 6)
                    pool.affine_select(out=causal2[:], in_=causal2[:], compare_op=ALU.is_ge, fill=-BIG, base=0,
                                       pattern=[[-SEQ, 2], [-1, SEQ]], channel_multiplier=1
                                       ).then_inc(q["masks_made"], 1)
                    for n, (base, pattern) in enumerate((
                            (0, [[0, PER_Q], [0, 4], [-1, 32]]), (-32, [[0, PER_Q], [0, 4], [-1, 32]]),
                            (-64, [[-4, PER_Q], [-1, 4], [0, 32]]), (-96, [[-4, PER_Q], [-1, 4], [0, 32]]))):
                        pool.affine_select(out=pick32[:], in_=pick32[:], compare_op=ALU.not_equal, fill=1.0,
                                           base=base, pattern=pattern, channel_multiplier=1
                                           ).then_inc(q["pick_made"], 1)
                        pool.wait_ge(q["pick_made"], n + 1)

                @block.tensor
                def _(pe):
                    pe.wait_ge(q["keys_in"], 16 * 5)
                    for h in range(HEADS):
                        for p in range(2):
                            last = nc.tensor.matmul(side[:, (h * 2 + p) * NK:(h * 2 + p + 1) * NK],
                                                    wqp[:, p * HEADS + h].rearrange("k a d -> k (a d)"),
                                                    keys[:, p * HEADS + h, :],
                                                    start=True, stop=True)
                    last.then_inc(q["score_w_ps"], 1)

                @block.vector
                def _(dve):
                    s = Steps(dve, q["mem_prep"])
                    dve.wait_ge(q["score_w_ps"], 1)
                    split(nc, s, score_w[:].rearrange("p a h k -> p a (h k)"), side[:])
                    dve.wait_ge(q["keys_in"], 16 * 5)
                    split(nc, s, wq_all, wq_in[:])
                    dve.wait_ge(q["masks_made"], 1)
                    for i in range(2):
                        hp = slice(i * SEQ, (i + 1) * SEQ)
                        s.did(nc.vector.tensor_copy(causal[hp, :], causal2[hp, i, :]))
                    dve.wait_ge(q["pick_made"], 4)
                    s.did(nc.vector.tensor_copy(lower[:], lower32[:]))
                    s.did(nc.vector.tensor_copy(pick[:].rearrange("p m (a b) -> p m a b", a=4), pick32[:]))
                    s.settle()


        hTb = sb("hTb", [P, BLK], F32R)
        score_wh = sb("score_wh", [P, 2, 2 * NK], F32R)
        wqh = sb("wqh", [P, 2, D], F32R)
        woh = [sb(f"woh{i}", [P, D]) for i in range(2)]
        sims = sb("sims", [P, TILES, 2 * NK])
        rest = [sb(f"rest{i}", [P, 2, 2, NK]) for i in range(2)]
        listed = sb("listed", [P, 2, TILES, LISTED])
        cand = sb("cand", [P, TILES, NCAND])
        cand_rest = [sb(f"cand_rest{i}", [P, 4, NCAND]) for i in range(2)]
        final = sb("final", [P, TILES, LISTED])
        mid = sb("mid", [P, TILES])
        neg_top = sb("neg_top", [P, TILES])
        neg_thr = sb("neg_thr", [P, TILES])
        over = sb("over", [P, TILES, TOPK])
        over_exp = sb("over_exp", [P, TILES, TOPK])
        kept = sb("kept", [P, TILES, TOPK])
        den = sb("den", [P, TILES])
        rden = [sb(f"rden{i}", [P, TILES]) for i in range(2)]
        thr_parts = sb("thr_parts", [P, 2, TILES], F32R)
        diag = sb("diag", [P, 2, TILES, P], F32R)
        hi = sb("hi", [P, BLK], F32R)
        lo = sb("lo", [P, BLK], F32R)
        scores = [sb(f"scores{i}", [P, QUARTERS, BLK], F32R) for i in range(2)]
        qT = [sb(f"qT{i}", [D, BLK]) for i in range(2)]
        table = sb("table", [P, QUARTERS, PER_Q, 2 * D])
        expo = [sb(f"expo{i}", [P, HALF]) for i in range(LAG + 1)]
        weight = [sb(f"weight{i}", [P, HALF]) for i in range(LAG + 1)]
        accS = sb("accS", [P, BLK])
        kv = sb("kv", [P, 2, TILES, D])
        kT = sb("kT", [D, BLK])
        masked = sb("masked", [P, TILES, SEQ])
        top1 = sb("top1", [P, TILES])
        shifted = sb("shifted", [P, TILES, SEQ])
        probsT = sb("probsT", [P, TILES, P])
        psumr = sb("psumr", [P, TILES])
        rsum = sb("rsum", [P, TILES])
        y = sb("y", [P, TILES, D])

        CREDIT = STEPS
        J_SIMS, J_KV, J_KT, J_LOGITS, J_PROBST, J_Y, J_Q, J_SCORES = 59, 5, 10, 15, 24, 31, 36, 51
        LIST_STEPS, FINAL_STEPS = 20, 10
        SELECT_STEPS = LIST_STEPS + 1 + FINAL_STEPS + 3
        SELECT_AT = [1 + 7 * n // 5 for n in range(SELECT_STEPS)]
        PREP_COUNT = 4 * 5 * 4 + len(CAND_BLOCKS) + 2 * 5 * 4 + 4 + 2
        ATTN_COUNT = 2 + 2
        def select_step(g):
            return SELECT_AT.index(g) if g in SELECT_AT else None

        with nc.Block() as block:
            @block.sync
            def _(sp):
                def load_quarter(v, at, c):
                    sp.wait_ge(q["w_used"], v * STEPS + (c + 1) * 2 * PER_Q)
                    sp.dma_start(table[:, c].rearrange("p m d -> p (m d)").unsqueeze(1),
                                 ins["table"][:, bass.ds(at * QUARTERS + c, 1), :]
                                 ).then_inc(table_in[c], 16)

                def send_scores(v, par):
                    sp.wait_ge(q["hi_ready"], v + 1)
                    sp.wait_ge(q["lo_ready"], v + 1)
                    for part, src in enumerate((hi, lo)):
                        for a in range(2):
                            sp.dma_start(
                                scores[par][32 * part:32 * part + 32, 2 * a:2 * a + 2, :].bitcast(F32),
                                spread(src[32 * a:32 * a + 32, :].bitcast(F32), 1, 2)
                            ).then_inc(scores_in[par], 16)
                            at = 64 + 32 * part
                            sp.dma_start(
                                scores[par][at:at + 32, a:a + 3:2, :].bitcast(F32),
                                spread(src[64 + 32 * a:96 + 32 * a, :].bitcast(F32), 1, 2)
                            ).then_inc(scores_in[par], 16)

                def load_unit(b, hp, par, first=False):
                    head = hp * 2 + par
                    v = b * HEADS + head
                    sp.wait_ge(q["scores_ps"], v + 1)
                    sp.dma_start(hTb[:].bitcast(F32), hT[:, bass.ds(b * BLK, BLK)].bitcast(F32)
                                 ).then_inc(q["staged"], 16)
                    sp.dma_start(score_wh[:].bitcast(F32).unsqueeze(2),
                                 score_w[:, :, bass.ds(head, 1), :].bitcast(F32)
                                 ).then_inc(q["staged"], 16)
                    sp.dma_start(wqh[:].bitcast(F32), wq_all[:, :, bass.ds(head * D, D)].bitcast(F32)
                                 ).then_inc(q["staged"], 16)
                    if not first:
                        send_scores(v - 1, 1 - par)
                        load_quarter(v - 1, head, QUARTERS - 1)
                    for c in range(QUARTERS - 1):
                        load_quarter(v, head + 1, c)
                        if c == 0:
                            sp.dma_start(woh[par][D:P, :].unsqueeze(1),
                                         ins["wo"][:, bass.ds(head, 1), :]).then_inc(q["wo_in"], 16)

                load_unit(0, 0, 0, first=True)
                load_unit(0, 0, 1)
                with sp.Fori(1, HEADS // 2) as hp:
                    for par in range(2):
                        load_unit(0, hp, par)
                with sp.Fori(1, NBLK) as b:
                    with sp.Fori(0, HEADS // 2) as hp:
                        for par in range(2):
                            load_unit(b, hp, par)
                send_scores(UNITS - 1, 1)
                load_quarter(UNITS - 1, HEADS, QUARTERS - 1)

            @block.gpsimd
            def _(pool):
                def make_diag(v):
                    pool.wait_ge(q["thr_ready"], v + 1)
                    for part in range(2):
                        pool.tensor_tensor(diag[:, part], spread(ident[:], 1, TILES),
                                           spread(thr_parts[:, part].bitcast(F32), 2, P),
                                           ALU.mult).then_inc(q["diag_ready"], 1)

                def add_output(b, w):
                    pool.wait_ge(q["y_ready"], w + 1)
                    pool.tensor_tensor(H[:, bass.ds(b * TILES, TILES), :], H[:, bass.ds(b * TILES, TILES), :],
                                       y[:], ALU.add).then_inc(q["y_added"], 1)
                    pool.wait_ge(q["y_added"], w + 1)

                make_diag(0)
                make_diag(1)
                with pool.Fori(0, NBLK - 1) as b:
                    with pool.Fori(0, HEADS) as h:
                        add_output(b, b * HEADS + h)
                        make_diag(b * HEADS + h + 2)
                with pool.Fori(0, HEADS - 2) as h:
                    add_output(NBLK - 1, h + (NBLK - 1) * HEADS)
                    make_diag(h + (NBLK - 1) * HEADS + 2)
                for h in range(HEADS - 2, HEADS):
                    add_output(NBLK - 1, (NBLK - 1) * HEADS + h)

            @block.tensor
            def _(pe):
                mm = nc.tensor.matmul

                def similarities(v):
                    pe.wait_ge(q["staged"], 48 * (v + 1))
                    if not (isinstance(v, int) and v == 0):
                        pe.wait_ge(q["lo_ready"], v)
                    for t in range(TILES):
                        for part in range(2):
                            last = mm(side[:, t * P:(t + 1) * P], hTb[:, t * P:(t + 1) * P],
                                      score_wh[:, part, :], start=part == 0, stop=part == 1)
                    last.then_inc(q["sims_ps"], 1)

                def queries(v):
                    pe.wait_ge(q["sims_ready"], v + 1)
                    if not (isinstance(v, int) and v < 2):
                        pe.wait_ge(q["y_ready"], v - 1)
                    hold(pe, core.passed)
                    for c in range(2):
                        cc = slice(c * HALF, (c + 1) * HALF)
                        for part in range(2):
                            last = mm(side[0:D, cc], wqh[:, part, :], hTb[:, cc],
                                      start=part == 0, stop=part == 1)
                    last.then_inc(q["q_ps"], 1)

                def thresholded(v):
                    pe.wait_ge(q["q_ready"], v + 1)
                    pe.wait_ge(q["diag_ready"], 2 * (v + 1))
                    for c in range(2):
                        cc = slice(c * HALF, (c + 1) * HALF)
                        for part in range(2):
                            mm(side[:, cc], score_wh[:, part, :], hTb[:, cc], start=part == 0, stop=False)
                        for part in range(2):
                            last = mm(side[:, cc], lower[:],
                                      diag[:, part, 4 * c:4 * c + 4].rearrange("p t k -> p (t k)"),
                                      start=False, stop=part == 1)
                    last.then_inc(q["scores_ps"], 1)

                def gathered(w, par):
                    pe.wait_ge(q["acc_copied"], w + 1)
                    pe.wait_ge(q["wo_in"], 16 * (w + 1))
                    if not (isinstance(w, int) and w >= UNITS - 2):
                        pe.wait_ge(q["sims_ready"], w + 3)
                    for t in range(TILES):
                        tt = slice(t * P, (t + 1) * P)
                        mm(side[:, HALF + t * D:HALF + (t + 1) * D], accS[D:P, tt], woh[par][D:P, :],
                           start=True, stop=True)
                        last = nc.tensor.transpose(side[:, t * D:(t + 1) * D], accS[0:D, tt], ident[0:D, 0:D])
                    last.then_inc(q["kv_ps"], 1)

                def keys_back(w):
                    pe.wait_ge(q["kv_ready"], 2 * (w + 1))
                    hold(pe, core.passed)
                    for t in range(TILES):
                        last = nc.tensor.transpose(side[0:D, t * P:(t + 1) * P], kv[:, 0, t, :], ident[:])
                    last.then_inc(q["kT_ps"], 1)

                def logits(w, par):
                    pe.wait_ge(q["kT_ready"], w + 1)
                    hold(pe, core.passed)
                    for t in range(TILES):
                        for i in range(2):
                            at = slice(t * P + i * SEQ, t * P + (i + 1) * SEQ)
                            last = mm(side[i * SEQ:(i + 1) * SEQ, t * SEQ:(t + 1) * SEQ],
                                      qT[par][:, at], kT[:, at], start=True, stop=True)
                    last.then_inc(q["logits_ps"], 1)

                def probs_transposed(w):
                    pe.wait_ge(q["probs_ready"], 2 * (w + 1))
                    for t in range(TILES):
                        last = nc.tensor.transpose(side[:, t * P:(t + 1) * P], probs[:, t, :], ident[:])
                    last.then_inc(q["probsT_ps"], 1)

                def attend(w):
                    pe.wait_ge(q["probsT_ready"], w + 1)
                    for t in range(TILES):
                        last = mm(side[:, t * D:(t + 1) * D], probsT[:, t, :], kv[:, 1, t, :],
                                  start=True, stop=True)
                    last.then_inc(q["y_ps"], 1)

                def product(u, g, begins=False):
                    k, half = divmod(g, 2)
                    pe.wait_ge(q["w_ready"], u * STEPS + (g + 1))
                    if g % (2 * PER_Q) == 0:
                        pe.wait_ge(table_in[k // PER_Q], 16 * (u + 1))
                    if g == 0 and not begins:
                        pe.wait_ge(q["acc_copied"], u)
                    mm(acc[:, half * HALF:(half + 1) * HALF], table[:, k // PER_Q, k % PER_Q, :],
                       weight[g % (LAG + 1)][:], start=k == 0, stop=k == CHUNKS - 1
                       ).then_inc(q["w_used"], 1)

                def unit(u, par, i, begins=False, attention=True, prepare=True, ahead=True):
                    for g in range(STEPS):
                        k, half = divmod(g, 2)
                        if g == 0:
                            pe.wait_ge(scores_in[par], 16 * 8 * (i + 1))
                        mm(psS[g % (LAG + 1)][:], pick[:, k % PER_Q, :],
                           scores[par][:, k // PER_Q, half * HALF:(half + 1) * HALF],
                           start=True, stop=True).then_inc(q["s_ready"], 1)
                        if g >= LAG:
                            product(u, g - LAG, begins)
                        elif not begins:
                            product(u - 1, STEPS + g - LAG)
                        if g == J_SIMS and ahead:
                            similarities(u + 2)
                        if attention:
                            if g == J_KV:
                                gathered(u - 1, 1 - par)
                            if g == J_KT:
                                keys_back(u - 1)
                            if g == J_LOGITS:
                                logits(u - 1, 1 - par)
                            if g == J_PROBST:
                                probs_transposed(u - 1)
                            if g == J_Y:
                                attend(u - 1)
                        if g == J_Q and prepare:
                            queries(u + 1)
                        if g == J_SCORES and prepare:
                            thresholded(u + 1)

                pe.sem_inc(q["w_used"], CREDIT)
                pe.sem_inc(q["scores_ps"], 1)
                similarities(0)
                queries(0)
                thresholded(0)
                similarities(1)
                unit(0, 0, 0, begins=True, attention=False)
                unit(1, 1, 0)
                with pe.Fori(1, PAIRS - 1) as i:
                    for par in range(2):
                        unit(i * 2 + par, par, i)
                unit(UNITS - 2, 0, PAIRS - 1, ahead=False)
                unit(UNITS - 1, 1, PAIRS - 1, prepare=False, ahead=False)
                for g in range(STEPS - LAG, STEPS):
                    product(UNITS - 1, g)
                gathered(UNITS - 1, 1)
                keys_back(UNITS - 1)
                logits(UNITS - 1, 1)
                probs_transposed(UNITS - 1)
                attend(UNITS - 1)

            @block.scalar
            def _(act):
                a = nc.scalar

                def copy_sims(v):
                    act.wait_ge(q["sims_ps"], v + 1)
                    a.copy(sims[:].rearrange("p t k -> p (t k)"), side[:]).then_inc(q["sims_ready"], 1)

                def exp_over(v):
                    act.wait_ge(q["exp_in"], v + 1)
                    a.activation(over_exp[:], over[:], ACT.Exp, bias=shift[:, 0:1]).then_inc(q["exp_done"], 1)

                def copy_queries(v, par):
                    act.wait_ge(q["q_ps"], v + 1)
                    a.activation(qT[par][:], side[0:D, :], ACT.Copy, scale=float(D) ** -0.5
                                 ).then_inc(q["q_ready"], 1)

                def high_parts(v, i_before, par_before):
                    act.wait_ge(q["scores_ps"], v + 2)
                    if i_before is not None:
                        act.wait_ge(scores_in[par_before], 16 * 8 * (i_before + 1))
                    a.copy(hi[:], side[:]).then_inc(q["hi_ready"], 1)

                def copy_acc(w):
                    act.wait_ge(q["w_used"], CREDIT + STEPS * (w + 1))
                    a.copy(accS[:], acc[:]).then_inc(q["acc_copied"], 1)

                def copy_kT(w):
                    act.wait_ge(q["kT_ps"], w + 1)
                    a.copy(kT[:], side[0:D, :]).then_inc(q["kT_ready"], 1)

                def exp_probs(w):
                    act.wait_ge(q["logits_ready"], w + 1)
                    for i in range(2):
                        at = slice(i * SEQ, (i + 1) * SEQ)
                        a.activation(probs[at, :, at], shifted[at], ACT.Exp).then_inc(q["probs_ready"], 1)

                def copy_probsT(w):
                    act.wait_ge(q["probsT_ps"], w + 1)
                    a.copy(probsT[:].rearrange("p t k -> p (t k)"), side[:]).then_inc(q["probsT_ready"], 1)

                def unit(u, par, i, begins=False, attention=True, prepare=True, ahead=True):
                    for g in range(STEPS):
                        act.wait_ge(q["s_ready"], u * STEPS + (g + 1))
                        a.activation(expo[g % (LAG + 1)][:], psS[g % (LAG + 1)][:], ACT.Exp,
                                     bias=shift[:, 0:1]).then_inc(q["e_ready"], 1)
                        if g == LAG - 1 and not begins:
                            copy_acc(u - 1)
                        if g == J_SIMS + 2 and ahead:
                            copy_sims(u + 2)
                        if attention:
                            if g == J_KT + 1:
                                copy_kT(u - 1)
                            if g == J_LOGITS + 4:
                                exp_probs(u - 1)
                            if g == J_PROBST + 1:
                                copy_probsT(u - 1)
                        if g == J_Q + 1 and prepare:
                            copy_queries(u + 1, 1 - par)
                        if g == J_SCORES + 1 and prepare:
                            high_parts(u + 1, i, par)
                        if g == J_SCORES + 3 and prepare:
                            exp_over(u + 1)

                copy_sims(0)
                copy_queries(0, 0)
                high_parts(0, None, None)
                exp_over(0)
                copy_sims(1)
                unit(0, 0, 0, begins=True, attention=False)
                unit(1, 1, 0)
                with act.Fori(1, PAIRS - 1) as i:
                    for par in range(2):
                        unit(i * 2 + par, par, i)
                unit(UNITS - 2, 0, PAIRS - 1, ahead=False)
                unit(UNITS - 1, 1, PAIRS - 1, prepare=False, ahead=False)
                copy_acc(UNITS - 1)
                copy_kT(UNITS - 1)
                exp_probs(UNITS - 1)
                copy_probsT(UNITS - 1)

            @block.vector
            def _(dve):
                v_ = nc.vector

                def sort_stage(s, stage, items):
                    for out, source, rest_a, rest_b in items:
                        if stage == 0:
                            s.did(v_.max(out[:, 0:8], source))
                        elif stage == 1:
                            s.did(v_.match_replace(rest_a, out[:, 0:8], source, -BIG))
                        elif stage == 2:
                            s.did(v_.max(out[:, 8:16], rest_a))
                        elif stage == 3:
                            s.did(v_.match_replace(rest_b, out[:, 8:16], rest_a, -BIG))
                        else:
                            s.did(v_.max(out[:, 16:24], rest_b))

                def select(s, n, v, par):
                    if n < LIST_STEPS:
                        group, stage = divmod(n, 5)
                        sort_stage(s, stage, [
                            (listed[:, p, t, :], sims[:, t, p * NK:(p + 1) * NK],
                             rest[0][:, t % 2, p, :], rest[1][:, t % 2, p, :])
                            for t in (2 * group, 2 * group + 1) for p in range(2)])
                    elif n == LIST_STEPS:
                        at = 0
                        for a0, na, nb in CAND_BLOCKS:
                            block_out = cand[:, :, at:at + na * nb].rearrange("p t (a b) -> p t a b", a=na)
                            s.did(v_.tensor_tensor(block_out, spread(listed[:, 0, :, a0:a0 + na], 3, nb),
                                                   spread(listed[:, 1, :, 0:nb], 2, na), ALU.add))
                            at += na * nb
                    elif n <= LIST_STEPS + FINAL_STEPS:
                        group, stage = divmod(n - LIST_STEPS - 1, 5)
                        sort_stage(s, stage, [
                            (final[:, t, :], cand[:, t, :], cand_rest[0][:, t % 4, :], cand_rest[1][:, t % 4, :])
                            for t in range(4 * group, 4 * group + 4)])
                    elif n == SELECT_STEPS - 3:
                        s.did(v_.tensor_tensor(mid[:], final[:, :, TOPK - 1], final[:, :, TOPK], ALU.add))
                        s.did(v_.tensor_scalar(neg_top[:], final[:, :, 0], -1.0, LOG_TINY, ALU.mult, ALU.add))
                        s.settle()
                        s.did(v_.scalar_tensor_tensor(neg_thr[:], mid[:], -0.5, neg_top[:],
                                                      ALU.mult, ALU.min))
                        s.settle()
                        s.did(v_.tensor_copy(thr_parts[:, 0], neg_thr[:]))
                        s.settle()
                        v_.tensor_tensor(thr_parts[:, 1], neg_thr[:], thr_parts[:, 0].bitcast(F32),
                                         ALU.subtract).then_inc(q["thr_ready"], 1)
                    elif n == SELECT_STEPS - 2:
                        v_.tensor_tensor(over[:], final[:, :, 0:TOPK], spread(neg_thr[:], 2, TOPK), ALU.add
                                         ).then_inc(q["exp_in"], 1)

                def denominators(s, v, par):
                    dve.wait_ge(q["exp_done"], v + 1)
                    s.did(v_.scalar_tensor_tensor(kept[:], over[:], 0.0, over_exp[:], ALU.is_ge, ALU.mult))
                    s.settle()
                    s.did(v_.reduce_sum(den[:], kept[:], axis=AX))
                    s.settle()
                    v_.reciprocal(rden[par][:], den[:])

                def low_parts(v):
                    dve.wait_ge(q["hi_ready"], v + 1)
                    v_.tensor_tensor(lo[:], side[:], hi[:].bitcast(F32), ALU.subtract).then_inc(q["lo_ready"], 1)

                def normalized(w, par, part):
                    if part == 0:
                        dve.wait_ge(q["kv_ps"], w + 1)
                    v_.tensor_tensor(kv[:, part], side[:, part * HALF:(part + 1) * HALF].rearrange(
                                         "p (t d) -> p t d", t=TILES),
                                     spread(rden[par][:], 2, D), ALU.mult).then_inc(q["kv_ready"], 1)

                def softmax_in(s, w):
                    dve.wait_ge(q["logits_ps"], w + 1)
                    s.did(v_.tensor_tensor(masked[:], side[:, 0:HALF].rearrange("p (t k) -> p t k", t=TILES),
                                           spread(causal[:], 1, TILES), ALU.add))
                    s.settle()
                    s.did(v_.reduce_max(top1[:], masked[:], axis=AX))
                    s.settle()
                    v_.tensor_tensor(shifted[:], masked[:], spread(top1[:], 2, SEQ), ALU.subtract
                                     ).then_inc(q["logits_ready"], 1)

                def softmax_sum(s, w):
                    dve.wait_ge(q["probs_ready"], 2 * (w + 1))
                    s.did(v_.reduce_sum(psumr[:], probs[:], axis=AX))
                    s.settle()
                    s.did(v_.reciprocal(rsum[:], psumr[:]))

                def output(s, w):
                    dve.wait_ge(q["y_ps"], w + 1)
                    s.settle()
                    v_.tensor_tensor(y[:], side[:, 0:HALF].rearrange("p (t d) -> p t d", t=TILES),
                                     spread(rsum[:], 2, D), ALU.mult).then_inc(q["y_ready"], 1)

                def unit(s, u, par, begins=False, attention=True, prepare=True):
                    for g in range(STEPS):
                        n = select_step(g) if prepare else None
                        if n == 0:
                            dve.wait_ge(q["sims_ready"], u + 2)
                        elif n is not None:
                            s.settle()
                        dve.wait_ge(q["e_ready"], u * STEPS + (g + 1))
                        v_.scalar_tensor_tensor(weight[g % (LAG + 1)][:], psS[g % (LAG + 1)][:], 0.0,
                                                expo[g % (LAG + 1)][:], ALU.is_ge, ALU.mult
                                                ).then_inc(q["w_ready"], 1)
                        if n is not None:
                            select(s, n, u + 1, 1 - par)
                        if attention:
                            if J_KV + 2 <= g <= J_KV + 3:
                                normalized(u - 1, 1 - par, g - J_KV - 2)
                            if g == J_LOGITS + 1:
                                softmax_in(s, u - 1)
                            if g == J_LOGITS + 7:
                                softmax_sum(s, u - 1)
                            if g == J_Y + 1:
                                output(s, u - 1)
                        if prepare:
                            if g == J_SCORES + 2:
                                low_parts(u + 1)
                            if g == J_SCORES + 5:
                                denominators(s, u + 1, 1 - par)

                COUNT = PREP_COUNT + ATTN_COUNT
                s = Steps(dve, q["mem_step"])
                dve.wait_ge(q["sims_ready"], 1)
                for n in range(SELECT_STEPS):
                    if n > 0:
                        s.settle()
                    select(s, n, 0, 0)
                low_parts(0)
                denominators(s, 0, 0)
                assert s.n == PREP_COUNT, s.n
                unit(s, 0, 0, begins=True, attention=False)
                unit(s, 1, 1)
                before = s.n
                assert before == 3 * PREP_COUNT + ATTN_COUNT, s.n
                with dve.Fori(1, PAIRS - 1) as i:
                    s = Steps(dve, q["mem_step"], i * (2 * COUNT) + (before - 2 * COUNT))
                    for par in range(2):
                        unit(s, i * 2 + par, par)
                    assert s.n == 2 * COUNT
                s = Steps(dve, q["mem_step"], before + (PAIRS - 2) * 2 * COUNT)
                unit(s, UNITS - 2, 0)
                unit(s, UNITS - 1, 1, prepare=False)
                for part in range(2):
                    normalized(UNITS - 1, 1, part)
                softmax_in(s, UNITS - 1)
                softmax_sum(s, UNITS - 1)
                dve.wait_ge(q["y_added"], UNITS - 1)
                output(s, UNITS - 1)


def recurrent(core):
    nc, ins = core.nc, core.inputs
    hT, H, ident, eps, row = core.hT, core.H, core.ident, core.eps, core.row
    with ExitStack() as scope:
        def sb(name, shape, dt=F32):
            return core.sb(name, shape, dt, scope)

        wi_in = sb("wi_in", [P, 2 * N])
        wiT = sb("wiT", [P, 2, 2 * N], F32R)
        bi = sb("bi", [N, 2])
        woT = sb("woT", [N, 2, D])
        plog = sb("plog", [N, 3])
        params = sb("params", [N, 3])
        wog = sb("wog", [N, 2, D])
        rate = sb("rate", [N, 1])
        decay = sb("decay_c", [N, IMG, SEQ])
        pos = sb("pos", [N, SEQ])
        angle = sb("angle", [N, SEQ])
        turns = sb("turns", [N, SEQ])
        red = sb("red", [N, SEQ])
        red2 = sb("red2", [N, SEQ])
        wrap = sb("wrap", [N, SEQ])
        cos = sb("cos", [N, SEQ])
        sin = sb("sin", [N, SEQ])
        z2 = sb("z2", [P, TILES, D])
        h2 = sb("h2", [P, TILES, D])
        h2b = sb("h2b", [P, TILES, D])
        h2T = sb("h2T", [P, BLK], F32R)
        ur = sb("ur", [N, IMG, SEQ])
        ui = sb("ui", [N, IMG, SEQ])
        vr = sb("vr", [N, IMG, SEQ])
        vi = sb("vi", [N, IMG, SEQ])
        t1 = sb("t1", [N, IMG, SEQ])
        t2 = sb("t2", [N, IMG, SEQ])
        yr = sb("yr", [N, IMG, SEQ])
        yi = sb("yi", [N, IMG, SEQ])
        xr = sb("xr", [N, IMG, SEQ])
        xi = sb("xi", [N, IMG, SEQ])
        z3 = sb("z3", [P, TILES, D])
        h3 = sb("h3", [P, TILES, D])
        norm2 = Norm(sb, "norm2")
        norm3 = Norm(sb, "norm3")
        ps_T = core.ps("ps_T2", [D, BLK], scope)
        ps_u = core.ps("ps_u", [N, 2, BLK], scope)
        ps_y = core.ps("ps_y", [P, TILES, D], scope)

        names = """rec_in rec_cleared rec_params rec_rate rec_trig rec_prep rec_angle rec_step z2_in
            squares2 root2 h2_ready h2T_ps h2_high h2T_ready u_ps u_ready v_pool scan_ready x_pool
            x_ready y3_ps squares3 root3 h3_ready h3T_ps h3_high h3_stored"""
        q = {n: core.sem(n) for n in names.split()}

        with nc.Block() as block:
            @block.sync
            def _(sp):
                for i in range(2):
                    sp.dma_start(wi_in[i * D:(i + 1) * D, :], ins["wiT"]).then_inc(q["rec_in"], 16)
                for dst, name in ((bi, "bi"), (woT, "woT"), (plog, "plog")):
                    sp.dma_start(dst[:], ins[name]).then_inc(q["rec_in"], 16)

            @block.gpsimd
            def _(pool):
                pool.memset(decay[:], 0.0).then_inc(q["rec_cleared"], 1)
                pool.iota(pos[:], pattern=[[1, SEQ]], base=0, channel_multiplier=0,
                          allow_small_or_imprecise_dtypes=True).then_inc(q["rec_cleared"], 1)

            @block.scalar
            def _(act):
                act.wait_ge(q["rec_in"], 16 * 5)
                nc.scalar.activation(params[:], plog[:], ACT.Exp).then_inc(q["rec_params"], 1)
                act.wait_ge(q["rec_params"], 1)
                nc.scalar.activation(rate[:], params[:, 0:1], ACT.Exp, scale=-1.0).then_inc(q["rec_rate"], 1)
                act.wait_ge(q["rec_angle"], 1)
                nc.scalar.activation(sin[:], red[:], ACT.Sin).then_inc(q["rec_trig"], 1)
                nc.scalar.activation(cos[:], wrap[:], ACT.Sin).then_inc(q["rec_trig"], 1)
                act.wait_ge(q["rec_trig"], 2)

            @block.vector
            def _(dve):
                v = nc.vector
                s = Steps(dve, q["rec_prep"])
                dve.wait_ge(q["rec_cleared"], 2)
                dve.wait_ge(q["rec_in"], 16 * 5)
                split(nc, s, wiT, wi_in[:])
                dve.wait_ge(q["rec_params"], 1)
                s.did(v.tensor_scalar(angle[:], pos[:], params[:, 1:2], None, ALU.mult))
                s.did(v.tensor_scalar(wog[:].rearrange("p a d -> p (a d)"),
                                      woT[:].rearrange("p a d -> p (a d)"), params[:, 2:3], None, ALU.mult))
                s.settle()
                ROUND = 12582912.0
                s.did(v.tensor_scalar(turns[:], angle[:], 1.0 / (2 * PI), ROUND, ALU.mult, ALU.add))
                s.settle()
                s.did(v.tensor_scalar(turns[:], turns[:], -ROUND, None, ALU.add))
                s.settle()
                parts = (6.28125, 0.0019340515136718750, 2 * PI - 6.28125 - 0.0019340515136718750)
                src, dst = angle, red
                for part in parts:
                    s.did(v.scalar_tensor_tensor(dst[:], turns[:], -part, src[:], ALU.mult, ALU.add))
                    s.settle()
                    src, dst = dst, (red2 if dst is red else red)
                assert src is red
                s.did(v.tensor_scalar(wrap[:], red[:], PI / 2, None, ALU.add))
                s.settle()
                s.did(v.tensor_scalar(red2[:], wrap[:], PI, -2 * PI, ALU.is_gt, ALU.mult))
                s.settle()
                s.did(v.tensor_tensor(wrap[:], wrap[:], red2[:], ALU.add))
                s.settle()
                s.did(v.tensor_scalar(wrap[:], wrap[:], PI_SAFE, -PI_SAFE, ALU.min, ALU.max))
                s.settle()
                v.tensor_scalar(red[:], red[:], PI_SAFE, -PI_SAFE, ALU.min, ALU.max).then_inc(q["rec_angle"], 1)
                dve.wait_ge(q["rec_rate"], 1)
                s.did(v.tensor_scalar(decay[:, :, 1:SEQ], decay[:, :, 1:SEQ], rate[:, 0:1], None, ALU.add))
                s.settle()

        FRONT, BACK = Norm.STEPS + 1, Norm.STEPS + 9
        LOOPED = NBLK - 1
        with nc.Block() as block:
            @block.tensor
            def _(pe):
                def features_in(b):
                    pe.wait_ge(q["h2_ready"], b + 1)
                    hold(pe, core.passed)
                    for t in range(TILES):
                        last = nc.tensor.transpose(ps_T[:, t * P:(t + 1) * P], h2[:, t, :], ident[:])
                    last.then_inc(q["h2T_ps"], 1)

                def project_in(b):
                    pe.wait_ge(q["h2T_ready"], b + 1)
                    for part in range(2):
                        for c in range(2):
                            cc = slice(c * HALF, (c + 1) * HALF)
                            for w in range(2):
                                last = nc.tensor.matmul(ps_u[:, part, cc], wiT[:, w, part * N:(part + 1) * N],
                                                        h2T[:, cc], start=w == 0, stop=w == 1)
                    last.then_inc(q["u_ps"], 1)

                def project_out(b):
                    pe.wait_ge(q["x_ready"], 2 * (b + 1))
                    for t in range(TILES):
                        for part, xx in enumerate((xr, xi)):
                            lhs = xx[:].rearrange("p i s -> p (i s)")[:, t * P:(t + 1) * P]
                            last = nc.tensor.matmul(ps_y[:, t, :], lhs, wog[:, part, :],
                                                    start=part == 0, stop=part == 1)
                    last.then_inc(q["y3_ps"], 1)

                def result_features(b):
                    pe.wait_ge(q["h3_ready"], b + 1)
                    hold(pe, core.passed)
                    for t in range(TILES):
                        last = nc.tensor.transpose(ps_T[:, t * P:(t + 1) * P], h3[:, t, :], ident[:])
                    last.then_inc(q["h3T_ps"], 1)

                features_in(0)
                project_in(0)
                with pe.Fori(0, LOOPED) as b:
                    features_in(b + 1)
                    project_out(b)
                    project_in(b + 1)
                    result_features(b)
                project_out(NBLK - 1)
                result_features(NBLK - 1)

            @block.scalar
            def _(act):
                def root2(b):
                    act.wait_ge(q["squares2"], b + 1)
                    norm2.root(nc, eps[:, 0:1]).then_inc(q["root2"], 1)

                def high2(b):
                    act.wait_ge(q["h2T_ps"], b + 1)
                    nc.scalar.copy(h2T[0:D, :], ps_T[:]).then_inc(q["h2_high"], 1)

                def inputs(b):
                    act.wait_ge(q["u_ps"], b + 1)
                    for part, uu in enumerate((ur, ui)):
                        nc.scalar.activation(uu[:].rearrange("p i s -> p (i s)"), ps_u[:, part, :],
                                             ACT.Identity, bias=bi[:, part:part + 1]).then_inc(q["u_ready"], 1)

                def root3(b):
                    act.wait_ge(q["squares3"], b + 1)
                    norm3.root(nc, eps[:, 0:1]).then_inc(q["root3"], 1)

                def high(b):
                    act.wait_ge(q["h3T_ps"], b + 1)
                    nc.scalar.copy(hT[0:D, bass.ds(b * BLK, BLK)], ps_T[:]).then_inc(q["h3_high"], 1)

                root2(0)
                high2(0)
                inputs(0)
                with act.Fori(0, LOOPED) as b:
                    root2(b + 1)
                    high2(b + 1)
                    root3(b)
                    inputs(b + 1)
                    high(b)
                root3(NBLK - 1)
                high(NBLK - 1)

            @block.gpsimd
            def _(pool):
                si = spread(sin[:], 1, IMG)

                def stage(b):
                    pool.tensor_copy(z2[:], H[:, bass.ds(b * TILES, TILES), :]).then_inc(q["z2_in"], 1)

                def iteration(b, last=False):
                    pool.wait_ge(q["u_ready"], 2 * (b + 1))
                    pool.tensor_tensor(t2[:], ur[:], si, ALU.mult).then_inc(q["v_pool"], 1)
                    if not last:
                        stage(b + 1)
                    pool.wait_ge(q["scan_ready"], 2 * (b + 1))
                    pool.tensor_tensor(t2[:], yr[:], si, ALU.mult).then_inc(q["x_pool"], 1)
                    pool.wait_ge(q["h3_ready"], b + 1)
                    hold(pool, core.passed)
                    pool.tensor_copy(H[:, bass.ds(b * TILES, TILES), :], h3[:]).then_inc(q["h3_stored"], 1)

                stage(0)
                with pool.Fori(0, LOOPED) as b:
                    iteration(b)
                iteration(NBLK - 1, last=True)

            @block.vector
            def _(dve):
                v = nc.vector
                ci, si = spread(cos[:], 1, IMG), spread(sin[:], 1, IMG)
                flat = "p i s -> p (i s)"

                def center2(s, b):
                    dve.wait_ge(q["z2_in"], b + 1)
                    norm2.center(nc, s, z2[:]).then_inc(q["squares2"], 1)

                def divide2(s, b):
                    dve.wait_ge(q["root2"], b + 1)
                    norm2.divide(nc, s, h2[:]).then_inc(q["h2_ready"], 1)

                def low2(b):
                    dve.wait_ge(q["h2_high"], b + 1)
                    v.tensor_tensor(h2T[D:P, :], ps_T[:], h2T[0:D, :].bitcast(F32), ALU.subtract
                                    ).then_inc(q["h2T_ready"], 1)

                def residual(s, b):
                    dve.wait_ge(q["h2_ready"], b + 1)
                    s.did(v.tensor_tensor(h2b[:], h2[:], spread(row["bo"], 1, TILES), ALU.add))

                def low(b):
                    dve.wait_ge(q["h3_high"], b + 1)
                    store_low(nc, hT, b, ps_T).then_inc(q["h3_stored"], 1)

                def iteration(s, b, first=False, last=False):
                    dve.wait_ge(q["u_ready"], 2 * (b + 1))
                    s.did(v.tensor_tensor(t1[:], ui[:], si, ALU.mult))
                    s.did(v.tensor_tensor(vr[:], ur[:], ci, ALU.mult))
                    s.did(v.tensor_tensor(vi[:], ui[:], ci, ALU.mult))
                    s.settle()
                    s.did(v.tensor_tensor(vr[:], vr[:], t1[:], ALU.add))
                    dve.wait_ge(q["v_pool"], b + 1)
                    s.did(v.tensor_tensor(vi[:], vi[:], t2[:], ALU.subtract))
                    s.settle()
                    for yy, vv in ((yr, vr), (yi, vi)):
                        v.tensor_tensor_scan(yy[:].rearrange(flat), decay[:].rearrange(flat),
                                             vv[:].rearrange(flat), 0.0, ALU.mult, ALU.add
                                             ).then_inc(q["scan_ready"], 1)
                    if not first:
                        low(b - 1)
                    if not last:
                        center2(s, b + 1)
                    dve.wait_ge(q["scan_ready"], 2 * (b + 1))
                    s.did(v.tensor_tensor(t1[:], yi[:], si, ALU.mult))
                    s.did(v.tensor_tensor(xr[:], yr[:], ci, ALU.mult))
                    s.did(v.tensor_tensor(xi[:], yi[:], ci, ALU.mult))
                    s.settle()
                    v.tensor_tensor(xr[:], xr[:], t1[:], ALU.subtract).then_inc(q["x_ready"], 1)
                    dve.wait_ge(q["x_pool"], b + 1)
                    v.tensor_tensor(xi[:], xi[:], t2[:], ALU.add).then_inc(q["x_ready"], 1)
                    if not last:
                        divide2(s, b + 1)
                        low2(b + 1)
                    dve.wait_ge(q["y3_ps"], b + 1)
                    s.did(v.tensor_tensor(z3[:], ps_y[:], h2b[:], ALU.add))
                    s.settle()
                    norm3.center(nc, s, z3[:]).then_inc(q["squares3"], 1)
                    if not last:
                        residual(s, b + 1)
                    dve.wait_ge(q["root3"], b + 1)
                    if not first:
                        dve.wait_ge(q["h3_stored"], 2 * b)
                    norm3.divide(nc, s, h3[:]).then_inc(q["h3_ready"], 1)

                s = Steps(dve, q["rec_step"])
                center2(s, 0)
                divide2(s, 0)
                low2(0)
                residual(s, 0)
                iteration(s, 0, first=True)
                before = s.n
                with dve.Fori(1, LOOPED) as b:
                    s = Steps(dve, q["rec_step"], before + (b - 1) * (FRONT + BACK))
                    iteration(s, b)
                    assert s.n == FRONT + BACK, s.n
                s = Steps(dve, q["rec_step"], before + (LOOPED - 1) * (FRONT + BACK))
                iteration(s, NBLK - 1, last=True)
                low(NBLK - 1)



def experts(core, out):
    nc, ins = core.nc, core.inputs
    hT, H, ident, eps, row = core.hT, core.H, core.ident, core.eps, core.row
    with ExitStack() as scope:
        def sb(name, shape, dt=F32):
            return core.sb(name, shape, dt, scope)

        gate_in = sb("gate_in", [P, EXP])
        gate_w = sb("gate_w", [P, 2, EXP], F32R)
        w1_in = sb("w1_in", [P, EXP, FF])
        w1 = sb("w1", [P, 2, EXP, FF], F32R)
        b1 = sb("b1e", [FF, EXP])
        w2 = sb("w2", [FF, EXP, D])
        b2 = sb("b2e", [EXP, D])
        xT = sb("xT", [P, BLK], F32R)
        lg = sb("lg", [P, TILES, EXP])
        best = sb("best", [P, TILES, 8])
        rel = sb("rel", [P, TILES, EXP])
        rel_exp = sb("rel_exp", [P, TILES, EXP])
        chosen = sb("chosen", [P, TILES, EXP])
        gate = sb("gate", [P, TILES, EXP])
        gsum = sb("gsum", [P, TILES])
        grec = sb("grec", [P, TILES])
        gateT = sb("gateT", [EXP, BLK])
        hidden = [sb(f"hidden{i}", [FF, EXP, HALF]) for i in range(2)]
        gated = [sb(f"gated{i}", [P, EXP, D]) for i in range(2)]
        moe = sb("moe", [P, TILES, D])
        base = sb("base", [P, TILES, D])
        z4 = sb("z4", [P, TILES, D])
        n4 = sb("n4", [P, TILES, D])
        n4g = sb("n4g", [P, TILES, D])
        n4b = sb("n4b", [P, TILES, D])
        z5 = sb("z5", [P, TILES, D])
        res = sb("res", [P, TILES, D])
        norm4 = Norm(sb, "norm4")
        norm5 = Norm(sb, "norm5")
        ps_g = core.ps("ps_g", [P, 512], scope)
        HBUF = 3
        ps_h = [core.ps(f"ps_h{i}", [FF, HALF], scope) for i in range(HBUF)]
        ps_e = [core.ps(f"ps_e{i}", [P, EXP, D], scope) for i in range(2)]

        names = """exp_w_in exp_split exp_step pool_step xT_ready gates_ps gates_in gates_exp gates_ready
            gateT_ps gateT_ready b2_ps base_ready hid_ps hid_ready exp_ps gated_ready squares4
            root4 n4_ready z5_ready squares5 root5 result_ready stored"""
        q = {n: core.sem(n) for n in names.split()}
        HPB = 2 * EXP
        SPB = 8
        PER_STEP = HPB // SPB
        V_GATES, V_TAIL = TILES + 5, 1 + 2 * Norm.STEPS
        V_FIRST = V_GATES + TILES // 2
        V_FULL = V_GATES + TILES + V_TAIL

        def rows_of(b):
            return H[:, bass.ds(b * TILES, TILES), :]

        def pe_hidden(pe, b, n):
            if n >= HBUF:
                pe.wait_ge(q["hid_ready"], b * HPB + (n - HBUF + 1))
            elif not (isinstance(b, int) and b == 0):
                pe.wait_ge(q["hid_ready"], b * HPB - (HPB % HBUF) + min(n + 1, HPB % HBUF))
            half, e = divmod(n, EXP)
            if e == 0 and half == 0:
                pe.wait_ge(q["xT_ready"], 2 * b + 1)
            for part in range(2):
                last = nc.tensor.matmul(ps_h[n % HBUF][:], w1[:, part, e, :],
                                        xT[:, half * HALF:(half + 1) * HALF],
                                        start=part == 0, stop=part == 1)
            last.then_inc(q["hid_ps"], 1)

        def pe_logits(pe, b, t, first):
            if t == 0:
                pe.wait_ge(q["xT_ready"], 2 * b + 2)
                if not first:
                    pe.wait_ge(q["base_ready"], b)
            for part in range(2):
                last = nc.tensor.matmul(ps_g[:, t * EXP:(t + 1) * EXP], xT[:, t * P:(t + 1) * P],
                                        gate_w[:, part, :], start=part == 0, stop=part == 1)
            if t == TILES - 1:
                last.then_inc(q["gates_ps"], 1)

        def pe_outputs(pe, b, t, quarters=range(4)):
            half = t // 4
            if quarters[0] == 0:
                if t % 4 == 0:
                    pe.wait_ge(q["hid_ready"], b * HPB + (half + 1) * EXP)
                if t >= 2 or not (isinstance(b, int) and b == 0):
                    pe.wait_ge(q["gated_ready"], b * TILES + (t - 1))
            for e in range(4 * quarters[0], 4 * (quarters[-1] + 1)):
                last = nc.tensor.matmul(ps_e[t % 2][:, e, :],
                                        hidden[half][:, e, (t % 4) * P:(t % 4 + 1) * P],
                                        w2[:, e, :], start=True, stop=True)
            if quarters[-1] == 3:
                last.then_inc(q["exp_ps"], 1)

        def pe_block(pe, b, first=False):
            for step in range(SPB):
                if step == 0:
                    for n in range(2 * PER_STEP):
                        pe_hidden(pe, b, n)
                for e in range(PER_STEP):
                    if step >= 2:
                        pe_hidden(pe, b, step * PER_STEP + e)
                    if step in (1, 2):
                        pe_logits(pe, b, (step - 1) * PER_STEP + e, first)
                    if e == PER_STEP - 1:
                        break
                    if step >= 4:
                        pe_outputs(pe, b, step - 4, (e,))
                    elif not first:
                        pe_outputs(pe, b - 1, step + 4, (e,))
                if step in (5, 6):
                    part = step - 5
                    if part == 0:
                        pe.wait_ge(q["gates_ready"], b + 1)
                    else:
                        pe.wait_ge(q["gateT_ready"], 2 * b + 1)
                    hold(pe, core.passed)
                    for t in range(4):
                        last = nc.tensor.transpose(ps_g[0:EXP, t * P:(t + 1) * P],
                                                   gate[:, part * 4 + t, :], ident[:])
                    last.then_inc(q["gateT_ps"], 1)
                if step == 7:
                    pe.wait_ge(q["gateT_ready"], 2 * b + 2)
                    for t in range(TILES):
                        last = nc.tensor.matmul(ps_g[:, t * D:(t + 1) * D], gateT[:, t * P:(t + 1) * P],
                                                b2[:], start=True, stop=True)
                    last.then_inc(q["b2_ps"], 1)
                if step >= 4:
                    pe_outputs(pe, b, step - 4, (3,))
                elif not first:
                    pe_outputs(pe, b - 1, step + 4, (3,))

        def act_root(act, norm, i, b):
            act.wait_ge(q[f"squares{i}"], b + 1)
            norm.root(nc, eps[:, 0:1]).then_inc(q[f"root{i}"], 1)

        def act_block(act, b, first=False):
            for n in range(HPB):
                half, e = divmod(n, EXP)
                act.wait_ge(q["hid_ps"], b * HPB + (n + 1))
                nc.scalar.activation(hidden[half][:, e, :], ps_h[n % HBUF][:], ACT.Relu,
                                     bias=b1[:, e:e + 1]).then_inc(q["hid_ready"], 1)
                if n == 16:
                    act.wait_ge(q["gates_in"], b + 1)
                    nc.scalar.activation(rel_exp[:], rel[:], ACT.Exp).then_inc(q["gates_exp"], 1)
                if n in (25, 29):
                    part = 0 if n == 25 else 1
                    act.wait_ge(q["gateT_ps"], 2 * b + (part + 1))
                    nc.scalar.copy(gateT[:, part * HALF:(part + 1) * HALF],
                                   ps_g[0:EXP, :]).then_inc(q["gateT_ready"], 1)
                if not first and n == 21:
                    act_root(act, norm4, 4, b - 1)
                if not first and n == 30:
                    act_root(act, norm5, 5, b - 1)

        def dve_outputs(dve, s, b, t):
            v = nc.vector
            dve.wait_ge(q["exp_ps"], b * TILES + (t + 1))
            v.tensor_tensor(gated[t % 2][:], ps_e[t % 2][:], spread(gate[:, t, :], 2, D),
                            ALU.mult).then_inc(q["gated_ready"], 1)
            dve.wait_ge(q["gated_ready"], b * TILES + (t + 1))
            s.did(v.reduce_sum(moe[:, t, :], gated[t % 2][:].rearrange("p e d -> p d e"), axis=AX))

        def dve_tail(dve, s, b, part):
            v = nc.vector
            if part == 0:
                s.settle()
                s.did(v.tensor_tensor(z4[:], base[:], moe[:], ALU.add))
                s.settle()
                norm4.center(nc, s, z4[:]).then_inc(q["squares4"], 1)
            elif part == 1:
                dve.wait_ge(q["root4"], b + 1)
                norm4.divide(nc, s, n4[:]).then_inc(q["n4_ready"], 1)
            elif part == 2:
                dve.wait_ge(q["z5_ready"], b + 1)
                norm5.center(nc, s, z5[:]).then_inc(q["squares5"], 1)
            else:
                dve.wait_ge(q["root5"], b + 1)
                if not (isinstance(b, int) and b == 0):
                    dve.wait_ge(q["stored"], 16 * b)
                norm5.divide(nc, s, res[:]).then_inc(q["result_ready"], 1)

        def dve_block(dve, b, first=False):
            v = nc.vector
            s = Steps(dve, q["exp_step"], 0 if first else V_FIRST + (b - 1) * V_FULL)
            if not first:
                dve_outputs(dve, s, b - 1, 4)
                dve_outputs(dve, s, b - 1, 5)
                dve_outputs(dve, s, b - 1, 6)
            dve.wait_ge(q["gates_ps"], b + 1)
            s.did(v.tensor_tensor(lg[:], ps_g[:, 0:TILES * EXP].rearrange("p (t e) -> p t e", e=EXP),
                                  spread(row["gate_b"], 1, TILES), ALU.add))
            s.settle()
            hold(dve, core.passed)
            for t in range(TILES):
                s.did(v.max(best[:, t, :], lg[:, t, :]))
            s.settle()
            v.tensor_tensor(rel[:], lg[:], spread(best[:, :, 0], 2, EXP), ALU.subtract
                            ).then_inc(q["gates_in"], 1)
            s.did(v.tensor_tensor(chosen[:], lg[:], spread(best[:, :, 1], 2, EXP), ALU.is_ge))
            if not first:
                dve_outputs(dve, s, b - 1, 7)
            s.settle()
            dve.wait_ge(q["gates_exp"], b + 1)
            s.did(v.tensor_tensor(chosen[:], chosen[:], rel_exp[:], ALU.mult))
            s.settle()
            s.did(v.reduce_sum(gsum[:], chosen[:], axis=AX))
            s.settle()
            s.did(v.reciprocal(grec[:], gsum[:]))
            s.settle()
            v.tensor_tensor(gate[:], chosen[:], spread(grec[:], 2, EXP), ALU.mult
                            ).then_inc(q["gates_ready"], 1)
            if not first:
                dve_tail(dve, s, b - 1, 0)
            dve.wait_ge(q["gates_ready"], b + 1)
            dve_outputs(dve, s, b, 0)
            if not first:
                dve_tail(dve, s, b - 1, 1)
            dve_outputs(dve, s, b, 1)
            dve_outputs(dve, s, b, 2)
            if not first:
                dve_tail(dve, s, b - 1, 2)
            dve.wait_ge(q["b2_ps"], b + 1)
            v.tensor_tensor(base[:], rows_of(b), ps_g[:].rearrange("p (t d) -> p t d", d=D), ALU.add
                            ).then_inc(q["base_ready"], 1)
            dve_outputs(dve, s, b, 3)
            if not first:
                dve_tail(dve, s, b - 1, 3)
            dve.wait_ge(q["base_ready"], b + 1)
            assert s.n == (V_FIRST if first else V_FULL), s.n

        with nc.Block() as block:
            @block.sync
            def _(sp):
                for dst, name in ((w1_in[0:D], "ew1"), (w1_in[D:P], "ew1"), (gate_in[0:D], "gate_w"),
                                  (gate_in[D:P], "gate_w"), (b1[:], "eb1"), (w2[:], "ew2"), (b2[:], "eb2")):
                    sp.dma_start(dst, ins[name]).then_inc(q["exp_w_in"], 16)
                with sp.Fori(0, NBLK) as b:
                    sp.wait_ge(q["result_ready"], b + 1)
                    sp.dma_start(out[:, bass.ds(b * TILES, TILES), :], res[:]).then_inc(q["stored"], 16)
                sp.wait_ge(q["stored"], 16 * NBLK)

            @block.gpsimd
            def _(pool):
                def gain_and_offset(b):
                    s = Steps(pool, q["pool_step"], 2 * b)
                    pool.wait_ge(q["n4_ready"], b + 1)
                    s.did(pool.tensor_tensor(n4g[:], n4[:], spread(row["ln_gamma"], 1, TILES), ALU.mult))
                    s.settle()
                    s.did(pool.tensor_tensor(n4b[:], n4g[:], spread(row["ln_beta"], 1, TILES), ALU.add))
                    s.settle()
                    pool.tensor_tensor(z5[:], n4b[:], rows_of(b), ALU.add).then_inc(q["z5_ready"], 1)

                for half in range(2):
                    pool.tensor_copy(xT[:, half * HALF:(half + 1) * HALF],
                                     hT[:, half * HALF:(half + 1) * HALF]).then_inc(q["xT_ready"], 1)
                with pool.Fori(1, NBLK) as b:
                    for half in range(2):
                        pool.wait_ge(q["hid_ps"], (b - 1) * HPB + (half + 1) * EXP)
                        hold(pool, core.passed)
                        pool.tensor_copy(xT[:, half * HALF:(half + 1) * HALF],
                                         hT[:, bass.ds(b * BLK + half * HALF, HALF)]
                                         ).then_inc(q["xT_ready"], 1)
                    gain_and_offset(b - 1)
                gain_and_offset(NBLK - 1)

            @block.tensor
            def _(pe):
                pe.wait_ge(q["exp_w_in"], 16 * 7)
                pe.wait_ge(q["exp_split"], 4)
                pe_block(pe, 0, first=True)
                with pe.Fori(1, NBLK) as b:
                    pe_block(pe, b)
                for t in range(4, TILES):
                    pe_outputs(pe, NBLK - 1, t)

            @block.scalar
            def _(act):
                act_block(act, 0, first=True)
                with act.Fori(1, NBLK) as b:
                    act_block(act, b)
                act_root(act, norm4, 4, NBLK - 1)
                act_root(act, norm5, 5, NBLK - 1)

            @block.vector
            def _(dve):
                dve.wait_ge(q["exp_w_in"], 16 * 7)
                s = Steps(dve, q["exp_split"])
                split(nc, s, w1[:].rearrange("p a e f -> p a (e f)"), w1_in[:].rearrange("p e f -> p (e f)"))
                split(nc, s, gate_w, gate_in[:])
                dve_block(dve, 0, first=True)
                with dve.Fori(1, NBLK) as b:
                    dve_block(dve, b)
                s = Steps(dve, q["exp_step"], V_FIRST + (NBLK - 1) * V_FULL)
                for t in range(4, TILES):
                    dve_outputs(dve, s, NBLK - 1, t)
                for part in range(4):
                    dve_tail(dve, s, NBLK - 1, part)


def kernel(**inputs):
    import numpy as np
    import concourse.bacc as bacc
    from concourse.bass_utils import run_bass_kernel_spmd

    a = {k: np.asarray(v) for k, v in inputs.items()}
    c = np.ascontiguousarray
    tab = np.concatenate([a["L0_ffn_keys_table"], a["L0_ffn_values_table"]], axis=1)
    tab = np.concatenate([tab[-NK * NK:], tab])
    tab = tab.reshape(HEADS + 1, 2, PER_Q, 4, 2, 32, 2 * D).transpose(3, 5, 0, 4, 1, 2, 6)
    wqpk = a["L0_ffn_Wq_pk"].reshape(D, 2 * HEADS, KD)
    pk = a["L0_ffn_pk_keys"]
    arrays = {
        "x": a["x"].reshape(TOK // P, P, D * 4).transpose(1, 0, 2),
        "tokw": np.concatenate([a["L0_tok_W"], a["L0_tok_b"][:, None]], axis=1),
        "cols": np.stack([a["L0_attn_" + n] for n in COLS], axis=1),
        "bmcm": np.stack([a["L0_attn_Bm"], a["L0_attn_Cm"]], axis=1),
        "taps": a["L0_attn_wd"].reshape(E, TAPS),
        "w1T": a["L0_attn_w1"].T,
        "w2T": a["L0_attn_w2"].T,
        "rows": np.concatenate([a["L0_attn_b2"], a["L1_attn_bo"], a["L1_ffn_gate_b"],
                                a["L1_ffn_gamma"], a["L1_ffn_beta"]])[None, :],
        "wqpkT": wqpk.transpose(2, 1, 0),
        "keysT": pk.transpose(3, 0, 2, 1).reshape(KD, 2 * HEADS, NK),
        "wq": a["L0_ffn_Wq"],
        "wo": a["L0_ffn_Wo"].reshape(HEADS, D, D).transpose(1, 0, 2),
        "table": tab.reshape(P, (HEADS + 1) * QUARTERS, PER_Q * 2 * D),
        "wiT": a["L1_attn_Wi"].T,
        "bi": a["L1_attn_bi"].reshape(2, N).T,
        "woT": a["L1_attn_Wo"].reshape(D, 2, N).transpose(2, 1, 0),
        "plog": a["L1_attn_params_log"].T,
        "gate_w": a["L1_ffn_gate_w"],
        "ew1": a["L1_ffn_w1"].transpose(1, 0, 2),
        "eb1": a["L1_ffn_b1"].T,
        "ew2": a["L1_ffn_w2"].transpose(1, 0, 2),
        "eb2": a["L1_ffn_b2"],
    }
    nc = bacc.Bacc("TRN2", target_bir_lowering=False, num_devices=1)
    feed, aps = {}, {}
    for name, value in arrays.items():
        feed["in_" + name] = c(value)
        aps[name] = nc.dram_tensor("in_" + name, value.shape, mybir.dt.from_np(value.dtype),
                                   kind="ExternalInput").ap()
    out = nc.dram_tensor("out_tokens", (P, TOK // P, D), F32, kind="ExternalOutput").ap()
    program(nc, aps, out)
    r = run_bass_kernel_spmd(nc, [feed], core_ids=[0])
    got = r.results[0]["out_tokens"]
    return np.ascontiguousarray(got.transpose(1, 0, 2)).reshape(IMAGES, SEQ, D)
```
